# Optimizing a Trainium2 kernel written in Bass

```python
import numpy as np
import jax
import jax.numpy as jnp

def _softmax(x, axis=-1):
    return jax.nn.softmax(x, axis=axis)

def _gelu(x):
    return jax.nn.gelu(x, approximate=True)

def _silu(x):
    return jax.nn.silu(x)

def _sigmoid(x):
    return jax.nn.sigmoid(x)

def _layernorm(x, axis=-1, eps=1e-05):
    m = jnp.mean(x, axis=axis, keepdims=True)
    v = jnp.var(x, axis=axis, keepdims=True)
    return (x - m) / jnp.sqrt(v + eps)

def _scatter_add(tgt, idx, src, axis=0):
    return tgt.at[idx].add(src)

def _segment_sum(src, seg, n):
    return jax.ops.segment_sum(src, seg, n)
kernel_name = 'mk_early_fusion_embed_d1_tok_img768_r4_4c2aba'

def setup_inputs(seed: int=0):
    np.random.seed(seed)
    _w = jnp.asarray

    def _rec_inputs():
        import jax
        import jax.numpy as jnp
        _rk = jax.random.key(seed)
        x = -0.000356955 + 1 * jax.random.normal(jax.random.fold_in(_rk, 1), (16, 3, 112, 112), jnp.float32)
        x_txt = jax.random.randint(jax.random.fold_in(_rk, 51), (16, 128), 0, 70, jnp.int32)
        return (x, x_txt)
    x, x_txt = _rec_inputs()

    def _L0_tok_setup():
        import jax, jax.numpy as jnp
        import numpy as np
        PATCH = 16
        EMBED = 192
        IN_DIM = PATCH * PATCH * 3

        def extract_patches(x, p):
            B, C, H, Wd = x.shape
            h, w = (H // p, Wd // p)
            xr = x.reshape(B, C, h, p, w, p)
            xr = xr.transpose(0, 2, 4, 3, 5, 1)
            return xr.reshape(B, h * w, p * p * C)
        key = jax.random.key(seed)
        kx, kw, kb = jax.random.split(key, 3)
        x = jax.random.normal(kx, (128, 3, 224, 224), dtype=jnp.float32)
        bound = 1.0 / np.sqrt(IN_DIM)
        W = jax.random.uniform(kw, (EMBED, IN_DIM), jnp.float32, -bound, bound)
        b = jax.random.uniform(kb, (EMBED,), jnp.float32, -bound, bound)
        return {'x': x, 'W': W, 'b': b}
    _L0_tok_all = _L0_tok_setup()
    _L0_tok_in = {k: v for k, v in _L0_tok_all.items() if k in ('W', 'b')}
    del _L0_tok_all

    def _L0_txt_setup():
        import jax, jax.numpy as jnp
        import numpy as np
        import math
        D_MODEL = 192
        BASE = D_MODEL // 3

        def positional_encoding(seq_length, d_model, dtype=jnp.float32):
            pos = jnp.arange(seq_length, dtype=dtype)[:, None]
            i_even = jnp.arange(0, d_model, 2, dtype=dtype)
            inv = jnp.exp(-(i_even / d_model) * math.log(10000.0))
            ang = pos * inv
            pe = jnp.stack([jnp.sin(ang), jnp.cos(ang)], axis=-1)
            return pe.reshape(seq_length, d_model)
        key = jax.random.key(seed)
        k_tok, k_c, k_s, k_q, k_sp = jax.random.split(key, 5)
        tokens = jax.random.randint(k_tok, (64, 512), 0, 70, dtype=jnp.int64)
        scale = 1.0
        color_W = jax.random.normal(k_c, (4, BASE), dtype=jnp.float32) * scale
        shape_W = jax.random.normal(k_s, (4, BASE), dtype=jnp.float32) * scale
        quantity_W = jax.random.normal(k_q, (4, BASE), dtype=jnp.float32) * scale
        special_W = jax.random.normal(k_sp, (6, D_MODEL), dtype=jnp.float32) * scale
        return {'tokens': tokens, 'color_W': color_W, 'shape_W': shape_W, 'quantity_W': quantity_W, 'special_W': special_W}
    _L0_txt_all = _L0_txt_setup()
    _L0_txt_in = {k: v for k, v in _L0_txt_all.items() if k in ('color_W', 'shape_W', 'quantity_W', 'special_W')}
    del _L0_txt_all

    def _L0_attn_setup():
        import jax, jax.numpy as jnp
        import numpy as np
        HIDDEN = 192
        HEADS = 12
        HEAD_DIM = HIDDEN // HEADS
        SCALE = HEAD_DIM ** (-0.5)
        GAMMA = 0.5

        def _spa_mask(N: int, dtype) -> jnp.ndarray:
            NUM = N // 4
            rows = jnp.arange(N) % NUM
            cols = jnp.arange(N) % NUM
            return jnp.where(rows[:, None] == cols[None, :], jnp.asarray(GAMMA, dtype), jnp.asarray(1.0, dtype))
        key = jax.random.key(seed)
        k1, k2, k3, k4 = jax.random.split(key, 4)
        B, N, C = (2, 512, HIDDEN)
        x = jax.random.normal(k1, (B, N, C), dtype=jnp.float32)
        w_qkv = jax.random.normal(k2, (3 * C, C), dtype=jnp.float32) * 0.02
        w_out = jax.random.normal(k3, (C, C), dtype=jnp.float32) * 0.02
        b_out = jax.random.normal(k4, (C,), dtype=jnp.float32) * 0.02
        return {'x': x, 'w_qkv': w_qkv, 'w_out': w_out, 'b_out': b_out}
    _L0_attn_all = _L0_attn_setup()
    _L0_attn_in = {k: v for k, v in _L0_attn_all.items() if k in ('w_qkv', 'w_out', 'b_out')}
    del _L0_attn_all

    def _L0_ffn_setup():
        import jax, jax.numpy as jnp
        import numpy as np
        B, S, H, D, E = (4, 512, 192, 256, 8)
        TOP_K = 2
        EPS = 1e-08
        LN_EPS = 1e-05

        def _gelu(t):
            return jax.nn.gelu(t, approximate=False)

        def _layer_norm(t, gamma, beta):
            mu = jnp.mean(t, axis=-1, keepdims=True)
            var = jnp.mean(jnp.square(t - mu), axis=-1, keepdims=True)
            return (t - mu) * jax.lax.rsqrt(var + LN_EPS) * gamma + beta
        key = jax.random.key(seed)
        ks = jax.random.split(key, 8)
        x = jax.random.normal(ks[0], (B, S, H), dtype=jnp.float32)
        w1 = jax.random.normal(ks[1], (H, H // 2), dtype=jnp.float32) * 0.02
        b1 = jnp.zeros((H // 2,), dtype=jnp.float32)
        w2 = jax.random.normal(ks[2], (H // 2, E), dtype=jnp.float32) * 0.02
        b2 = jnp.zeros((E,), dtype=jnp.float32)
        a_dn = float(np.sqrt(6.0 / (H + D)))
        a_up = float(np.sqrt(6.0 / (D + H)))
        down_w = jax.random.uniform(ks[3], (E, H, D), dtype=jnp.float32, minval=-a_dn, maxval=a_dn)
        down_b = jnp.zeros((E, D), dtype=jnp.float32)
        up_w = jax.random.uniform(ks[4], (E, D, H), dtype=jnp.float32, minval=-a_up, maxval=a_up)
        gamma = jnp.ones((H,), dtype=jnp.float32)
        beta = jnp.zeros((H,), dtype=jnp.float32)
        return {'x': x, 'w1': w1, 'b1': b1, 'w2': w2, 'b2': b2, 'down_w': down_w, 'down_b': down_b, 'up_w': up_w, 'gamma': gamma, 'beta': beta}
    _L0_ffn_all = _L0_ffn_setup()
    _L0_ffn_in = {k: v for k, v in _L0_ffn_all.items() if k in ('w1', 'b1', 'w2', 'b2', 'down_w', 'down_b', 'up_w', 'gamma', 'beta')}
    del _L0_ffn_all
    return {'x': x, 'x_txt': x_txt, 'L0_tok_W': _L0_tok_in['W'], 'L0_tok_b': _L0_tok_in['b'], 'L0_txt_color_W': _L0_txt_in['color_W'], 'L0_txt_shape_W': _L0_txt_in['shape_W'], 'L0_txt_quantity_W': _L0_txt_in['quantity_W'], 'L0_txt_special_W': _L0_txt_in['special_W'], 'L0_attn_w_qkv': _L0_attn_in['w_qkv'], 'L0_attn_w_out': _L0_attn_in['w_out'], 'L0_attn_b_out': _L0_attn_in['b_out'], 'L0_ffn_w1': _L0_ffn_in['w1'], 'L0_ffn_b1': _L0_ffn_in['b1'], 'L0_ffn_w2': _L0_ffn_in['w2'], 'L0_ffn_b2': _L0_ffn_in['b2'], 'L0_ffn_down_w': _L0_ffn_in['down_w'], 'L0_ffn_down_b': _L0_ffn_in['down_b'], 'L0_ffn_up_w': _L0_ffn_in['up_w'], 'L0_ffn_gamma': _L0_ffn_in['gamma'], 'L0_ffn_beta': _L0_ffn_in['beta']}

def reference(x, x_txt, L0_tok_W, L0_tok_b, L0_txt_color_W, L0_txt_shape_W, L0_txt_quantity_W, L0_txt_special_W, L0_attn_w_qkv, L0_attn_w_out, L0_attn_b_out, L0_ffn_w1, L0_ffn_b1, L0_ffn_w2, L0_ffn_b2, L0_ffn_down_w, L0_ffn_down_b, L0_ffn_up_w, L0_ffn_gamma, L0_ffn_beta):
    import jax
    import jax.numpy as jnp

    def _L0_tok_ref(x, W, b):
        import jax, jax.numpy as jnp
        import numpy as np
        PATCH = 16
        EMBED = 192
        IN_DIM = PATCH * PATCH * 3

        def extract_patches(x, p):
            B, C, H, Wd = x.shape
            h, w = (H // p, Wd // p)
            xr = x.reshape(B, C, h, p, w, p)
            xr = xr.transpose(0, 2, 4, 3, 5, 1)
            return xr.reshape(B, h * w, p * p * C)
        patches = extract_patches(x, PATCH)
        return jnp.einsum('bnd,ed->bne', patches, W) + b

    def _L0_txt_ref(tokens, color_W, shape_W, quantity_W, special_W):
        import jax, jax.numpy as jnp
        import numpy as np
        import math
        D_MODEL = 192
        BASE = D_MODEL // 3

        def positional_encoding(seq_length, d_model, dtype=jnp.float32):
            pos = jnp.arange(seq_length, dtype=dtype)[:, None]
            i_even = jnp.arange(0, d_model, 2, dtype=dtype)
            inv = jnp.exp(-(i_even / d_model) * math.log(10000.0))
            ang = pos * inv
            pe = jnp.stack([jnp.sin(ang), jnp.cos(ang)], axis=-1)
            return pe.reshape(seq_length, d_model)
        B, S = tokens.shape
        d_model = special_W.shape[1]
        t = jnp.minimum(tokens, 63)
        color = t // 16
        shape = t % 16 // 4
        quantity = t % 4
        feat_emb = jnp.concatenate([color_W[color], shape_W[shape], quantity_W[quantity]], axis=-1)
        sp_idx = jnp.clip(tokens - 64, 0, special_W.shape[0] - 1)
        spec_emb = special_W[sp_idx]
        emb = jnp.where((tokens < 64)[..., None], feat_emb, spec_emb)
        pe = positional_encoding(S, d_model, dtype=emb.dtype)
        out = emb * jnp.asarray(math.sqrt(d_model), emb.dtype) + pe[None, :, :]
        return out

    def _L0_attn_ref(x, w_qkv, w_out, b_out):
        import jax, jax.numpy as jnp
        import numpy as np
        HIDDEN = 192
        HEADS = 12
        HEAD_DIM = HIDDEN // HEADS
        SCALE = HEAD_DIM ** (-0.5)
        GAMMA = 0.5

        def _spa_mask(N: int, dtype) -> jnp.ndarray:
            NUM = N // 4
            rows = jnp.arange(N) % NUM
            cols = jnp.arange(N) % NUM
            return jnp.where(rows[:, None] == cols[None, :], jnp.asarray(GAMMA, dtype), jnp.asarray(1.0, dtype))
        B, N, C = x.shape
        H, D = (HEADS, HEAD_DIM)
        qkv = jnp.einsum('bnc,fc->bnf', x, w_qkv).reshape(B, N, 3, H, D)
        qkv = jnp.transpose(qkv, (2, 0, 3, 1, 4))
        q, k, v = (qkv[0], qkv[1], qkv[2])
        att = jax.nn.softmax(jnp.einsum('bhxd,bhyd->bhxy', q, k) * SCALE, axis=-1)
        mask = _spa_mask(N, att.dtype)
        att = jax.nn.softmax(att * mask, axis=-1)
        out = jnp.einsum('bhxy,bhyd->bhxd', att, v)
        out = jnp.transpose(out, (0, 2, 1, 3)).reshape(B, N, C)
        return jnp.einsum('bnc,oc->bno', out, w_out) + b_out

    def _L0_ffn_ref(x, w1, b1, w2, b2, down_w, down_b, up_w, gamma, beta):
        import jax, jax.numpy as jnp
        import numpy as np
        B, S, H, D, E = (4, 512, 192, 256, 8)
        TOP_K = 2
        EPS = 1e-08
        LN_EPS = 1e-05

        def _gelu(t):
            return jax.nn.gelu(t, approximate=False)

        def _layer_norm(t, gamma, beta):
            mu = jnp.mean(t, axis=-1, keepdims=True)
            var = jnp.mean(jnp.square(t - mu), axis=-1, keepdims=True)
            return (t - mu) * jax.lax.rsqrt(var + LN_EPS) * gamma + beta
        logits = _gelu(x @ w1 + b1) @ w2 + b2
        routing = jax.nn.softmax(logits, axis=-1)
        topv, topi = jax.lax.top_k(routing, TOP_K)
        sparse = jnp.sum(jax.nn.one_hot(topi, E, dtype=routing.dtype) * topv[..., None], axis=-2)
        sparse = sparse / (jnp.sum(sparse, axis=-1, keepdims=True) + EPS)
        z = _gelu(jnp.einsum('bsh,ehd->bsed', x, down_w) + down_b)
        expert_out = jnp.einsum('bsed,edh->bseh', z, up_w)
        moe_out = jnp.einsum('bseh,bse->bsh', expert_out, sparse)
        return _layer_norm(x + moe_out, gamma, beta)
    h = _L0_tok_ref(x, L0_tok_W, L0_tok_b)
    h = jnp.concatenate([h, _L0_txt_ref(x_txt, L0_txt_color_W, L0_txt_shape_W, L0_txt_quantity_W, L0_txt_special_W)], axis=1)
    h = h + _L0_attn_ref(_layernorm(h, axis=-1), L0_attn_w_qkv, L0_attn_w_out, L0_attn_b_out)
    h = h + _L0_ffn_ref(_layernorm(h, axis=-1), L0_ffn_w1, L0_ffn_b1, L0_ffn_w2, L0_ffn_b2, L0_ffn_down_w, L0_ffn_down_b, L0_ffn_up_w, L0_ffn_gamma, L0_ffn_beta)
    return h

_drawn_inputs = setup_inputs


def setup_inputs(seed=0):
    import zlib

    import numpy as np

    out = dict(_drawn_inputs(seed))
    spreads = {'L0_ffn_b1': (0.0, 0.398),
     'L0_ffn_b2': (0.0, 0.1),
     'L0_ffn_down_b': (0.0, 0.8),
     'L0_ffn_gamma': (1.0, 0.6),
     'L0_ffn_beta': (0.0, 0.8)}
    factors = {'L0_tok_b': 8.0,
     'L0_attn_w_qkv': 8.0,
     'L0_attn_w_out': 8.0,
     'L0_attn_b_out': 24.868,
     'L0_ffn_w1': 3.09,
     'L0_ffn_w2': 2.83}
    for name, (base, spread) in spreads.items():
        noise = np.random.default_rng([zlib.crc32(name.encode()), seed]).standard_normal(out[name].shape)
        drawn = base * np.exp(spread * noise) if base else spread * noise
        out[name] = jnp.asarray(drawn.astype(out[name].dtype))
    for name, factor in factors.items():
        out[name] = (out[name] * factor).astype(out[name].dtype)
    return out
```

```python
from contextlib import ExitStack

import numpy as np

import concourse.bass as bass
from concourse import mybir

F32 = mybir.dt.float32
BF16 = mybir.dt.bfloat16
I32 = mybir.dt.int32
ALU = mybir.AluOpType
ACT = mybir.ActivationFunctionType
AX_X = mybir.AxisListType.X

B = 16
NI, NT = 49, 128
N = NI + NT
T = B * N
C = 192
CP = C // 2
H, D = 12, 16
NUM = N // 4
KP = 6
NPATCH = B * NI
VOC = 70
E, ED = 8, 256
LN_EPS = 1e-5
GATE_EPS = 1e-8

BLK = 472
NBLK = T // BLK
TT = 118
SUB = BLK // TT
TPAD = T + 16

QW = 192
REST = N - 128
PW = 64 + REST
UNITS = 3
PAIRS = H // 2
NPAIR = B * PAIRS
PER = 2 * PAIRS
NIT = NPAIR // PER
GROUPS = PAIRS // 2
T0W = 128 + PW + 128
AT1 = 192
AT2 = AT1 + N
ATW = AT2 + 192
DRAIN = 5

Q_PART = [0, 0, 0, 1, 1, 1, 2, 2]
K_PART = [0, 1, 2, 0, 1, 2, 0, 1]


def wait(eng, sem, value):
    if not (isinstance(value, int) and value <= 0):
        eng.wait_ge(sem, value)


def pair_steps(first, last):
    return range(-2 if first else 0, PER + (DRAIN if last else 0))


def looped(eng, body):
    body(0, True, False)
    with eng.Fori(1, NIT - 1, 1) as it:
        body(it, False, False)
    body(NIT - 1, False, True)


def build(nc, a, out):
    with ExitStack() as ctx:
        def sb(name, shape, dt=F32):
            return ctx.enter_context(nc.sbuf_tensor(name, shape, dt))

        def sem(name):
            return ctx.enter_context(nc.semaphore(name))

        bank = [ctx.enter_context(nc.psum_tensor(f"bank{i}", [128, 512], F32)) for i in range(8)]
        parts_dram = nc.dram_tensor("qk_parts", (3, 2 * C, TPAD), BF16).ap()

        hT = sb("hT", [CP, 2, T])
        hn = sb("hn", [CP, 2, TPAD])
        w_tok = sb("w_tok", [128, KP, C])
        b_tok = sb("b_tok", [CP, 2])
        table = sb("table", [VOC, C])
        iota = sb("iota", [VOC, 1])
        pe_sb = sb("pe_sb", [CP, 2, NT])
        neg_half = sb("neg_half", [128, 1])
        eps = sb("eps", [TT, 1])
        one = sb("one", [128, 1])
        w_qk = sb("w_qk", [CP, 2, 2 * C])
        qk_scale = sb("qk_scale", [128, 3])
        w_v = sb("w_v", [CP, 2, C])
        w_o = sb("w_o", [128, GROUPS, C])
        b_o = sb("b_o", [CP, 2])
        ident = sb("ident", [128, 128])
        mask_a = sb("mask_a", [128, N])
        mask_r = sb("mask_r", [128, N])
        mask_b = sb("mask_b", [128, N])
        w1 = sb("w1", [CP, 2, CP])
        b1 = sb("b1", [CP, 1])
        w2 = sb("w2", [CP, E])
        b2 = sb("b2", [TT, E])
        earlier = sb("earlier", [TT, E, E])
        down_b = sb("down_b", [128, 2 * E])
        gamma = sb("gamma", [TT, C])
        beta = sb("beta", [TT, C])
        zero = sb("zero", [128, 16], BF16)

        area_a = sb("area_a", [128, 8960])
        area_b = sb("area_b", [128, 7168])
        area_c = sb("area_c", [128, 7264])

        def carve(area, at, shape, dt=F32):
            n = int(np.prod(shape[1:]))
            words = n if dt is not BF16 else n // 2
            v = area[0:shape[0], at:at + words]
            if dt is not F32:
                v = v.bitcast(dt)
            names = ["x", "y", "z"][:len(shape) - 1]
            if len(names) > 1:
                v = v.rearrange(f"p ({' '.join(names)}) -> p {' '.join(names)}",
                                **dict(zip(names[1:], shape[2:])))
            return v, at + words

        x_patch, o = carve(area_a, 0, [128, KP, NPATCH])
        tok_i, o = carve(area_a, o, [VOC, B * NT], I32)
        onehot, o = carve(area_a, o, [VOC, B * NT])
        q_st, k_st, o = [None] * 2, [None] * 2, 0
        for u in range(2):
            q_st[u], o = carve(area_a, o, [128, H, QW], BF16)
            k_st[u], o = carve(area_a, o, [128, H, N], BF16)
        part, o = [None] * 2, 0
        rest = [None] * 2
        for u in range(2):
            part[u], o = carve(area_b, o, [128, 9, BLK], BF16)
            rest[u], o = carve(area_b, o, [128, 3, BLK])
        w_down, o = carve(area_b, 0, [CP, 2, E * ED])
        w_up, o = carve(area_b, o, [128, 2 * E, C])
        NTILE = NBLK * SUB
        h2b, o = carve(area_a, 0, [TT, NTILE, C])
        xn, o = carve(area_c, 0, [TT, NTILE, C])
        z = [None] * 2
        for u in range(2):
            z[u], o = carve(area_c, o, [128, 2, BLK])
        acc, o = carve(area_c, o, [TT, SUB, C])
        y_out = sb("y_out", [TT, SUB, C])
        n_stats = sb("n_stats", [TT, NTILE, 6])
        n_mv = sb("n_mv", [TT, NTILE, 2])
        n_var = sb("n_var", [TT, NTILE])
        n_rstd = sb("n_rstd", [TT, NTILE])

        hn_b = [sb(f"hn_b{u}", [CP, 2, QW]) for u in range(2)]
        v_lo = [sb(f"v_lo{u}", [128, H, 2 * D]) for u in range(2)]
        v_hi = [sb(f"v_hi{u}", [128, H, 2 * D]) for u in range(2)]
        neg_max = [sb(f"neg_max{u}", [128, UNITS]) for u in range(2)]
        e1 = [sb(f"e1_{u}", [128, UNITS, N]) for u in range(2)]
        sum1 = [sb(f"sum1_{u}", [128, UNITS]) for u in range(2)]
        rsum1 = [sb(f"rsum1_{u}", [128, UNITS]) for u in range(2)]
        att = [sb(f"att{u}", [128, ATW]) for u in range(2)]
        p_lo = [sb(f"p_lo{u}", [128, T0W]) for u in range(4)]
        p_hi = [sb(f"p_hi{u}", [128, N]) for u in range(4)]
        o_raw = [sb(f"o_raw{u}", [128, N]) for u in range(2)]
        rsum2 = sb("rsum2", [128, 2, 4])
        rsum2_rep = sb("rsum2_rep", [128, 2, 4, 2 * D])
        o_norm = [sb(f"o_norm{u}", [128, GROUPS, N]) for u in range(2)]

        g1 = [sb(f"g1_{u}", [CP, BLK]) for u in range(2)]
        logit = sb("logit", [TT, NBLK * SUB, E])
        cmp_ge, _ = carve(area_c, NTILE * C, [TT, NTILE, E, E])
        cmp_gt = sb("cmp_gt", [TT, NTILE, E, E])
        top = sb("top", [TT, NTILE])
        rank = sb("rank", [TT, NTILE, E])
        shifted = sb("shifted", [TT, NTILE, E])
        expl = sb("expl", [TT, NTILE, E])
        kept = sb("kept", [TT, NTILE, E])
        sum_k = sb("sum_k", [TT, NTILE])
        sum_e = sb("sum_e", [TT, NTILE])
        gate = sb("gate", [TT, NTILE, E])
        gate_b = sb("gate_b", [TT, SUB, E])
        stats = sb("stats", [TT, SUB, 6])
        mv = sb("mv", [TT, SUB, 2])
        rstd_y = sb("rstd_y", [TT, SUB])
        vy = sb("vy", [TT, SUB])

        patch_in, text_in, const_in = sem("patch_in"), sem("text_in"), sem("const_in")
        expert_w_in = sem("expert_w_in")
        preset = sem("preset")
        zeroed = sem("zeroed")
        onehot_done, embed_mm, embed_img, embed_txt = (sem(n) for n in
            ("onehot_done", "embed_mm", "embed_img", "embed_txt"))
        h_tp, n_stat, n_mv_done, n_var_done, n_rstd_done, xn_done, xn_tp, hn_done, h2_out, h2b_done = (
            sem(n) for n in ("h_tp", "n_stat", "n_mv_done", "n_var_done", "n_rstd_done", "xn_done", "xn_tp",
                             "hn_done", "h2_out", "h2b_done"))
        qk_mm, part_a, rest_a, part_b, part_c, pad_stored = (sem(n) for n in
            ("qk_mm", "part_a", "rest_a", "part_b", "part_c", "pad_stored"))
        parts_stored = [sem(f"parts_stored{u}") for u in range(2)]
        hnb_in = [sem(f"hnb_in{u}") for u in range(2)]
        stack_in = [sem(f"stack_in{u}") for u in range(2)]
        s_mm_b, s_mm, max_b, max_done, exp1_b, exp1_a, rsum_done, att_done, tr_mm, exp2_done, pv_mm = (sem(n) for n in
            ("s_mm_b", "s_mm", "max_b", "max_done", "exp1_b", "exp1_a", "rsum_done", "att_done", "tr_mm", "exp2_done", "pv_mm"))
        v_mm, v_out, o_out, sum2_tp, rsum2_done, rep_done, rsum2_tp, onorm_done, proj_mm, h_added = (sem(n) for n in
            ("v_mm", "v_out", "o_out", "sum2_tp", "rsum2_done", "rep_done", "rsum2_tp", "onorm_done", "proj_mm", "h_added"))
        g1_mm, g1_done, logit_mm, logit_done, route_dve, route_exp = (sem(n) for n in
            ("g1_mm", "g1_done", "logit_mm", "logit_done", "route_dve", "route_exp"))
        down_mm, z_done, up_mm, acc_done = (sem(n) for n in
            ("down_mm", "z_done", "up_mm", "acc_done"))
        gate_cp, fin_dve, stats_seen, mv_done, vy_done, rstdy_done, y_done, y_stored = (sem(n) for n in
            ("gate_cp", "fin_dve", "stats_seen", "mv_done", "vy_done", "rstdy_done", "y_done", "y_stored"))

        block = ctx.enter_context(nc.Block())
        IMG_BLKS, IMG_N = 2, NPATCH // 2
        TXT_BLKS, TXT_B = 4, 4

        def batches_before(tokens):
            return -(-tokens // N)

        def blk(t, n, width=BLK):
            return t[:, :, bass.ds(n * BLK, width)]

        CONSTS = 25

        @block.sync
        def _(sp):
            def load(dst, src, s):
                sp.dma_start(dst, src).then_inc(s, 16)

            load(w_tok[:], a["w_tok"], patch_in)
            load(b_tok[:], a["b_tok"], patch_in)
            for k in range(KP):
                load(x_patch[:, k, :], a["x_patch"][:, k, :], patch_in)
            load(tok_i, a["tokens"].partition_broadcast(VOC), text_in)
            for i in range(4):
                load(table[16 * i:16 * i + 16, 0:64], a["color"][i, :].partition_broadcast(16), text_in)
            for i in range(16):
                load(table[4 * i:4 * i + 4, 64:128], a["shape"][i % 4, :].partition_broadcast(4), text_in)
                load(table[4 * i:4 * i + 4, 128:C], a["quantity"], text_in)
            load(table[64:VOC, :], a["special"], text_in)
            load(iota[:], a["iota"], text_in)
            load(pe_sb[:], a["pe"], text_in)
            for dst, name in ((neg_half, "neg_half"), (eps, "eps"), (w_qk, "w_qk"),
                              (qk_scale, "qk_scale"), (w_v, "w_v"), (w_o, "w_o"), (b_o, "b_o"),
                              (ident, "ident"), (mask_a, "mask_a"), (mask_b, "mask_b"), (mask_r, "mask_r"),
                              (w1, "w1"),
                              (b1, "b1"), (w2, "w2"), (earlier, "earlier"), (down_b, "down_b")):
                load(dst[:], a[name], const_in)
            load(b2[:], a["b2"].partition_broadcast(TT), const_in)
            load(gamma[:], a["gamma"].partition_broadcast(TT), const_in)
            load(beta[:], a["beta"].partition_broadcast(TT), const_in)

            sp.wait_ge(preset, 1)
            for t in range(9):
                load(parts_dram[t // 3, 128 * (t % 3):128 * (t % 3) + 128, T:TPAD], zero[:], pad_stored)
            for n in range(NBLK):
                sp.wait_ge(part_c, 3 * n + 3)
                for k in range(3):
                    load(parts_dram[k, :, n * BLK:(n + 1) * BLK].rearrange("(t p) n -> p t n", p=128),
                         part[n % 2][:, 3 * k:3 * k + 3, :], parts_stored[n % 2])

            sp.wait_ge(hn_done, NBLK)
            for u in range(2):
                sp.wait_ge(parts_stored[u], 48 * NBLK // 2)
            sp.wait_ge(pad_stored, 16 * 9)
            sp.wait_ge(embed_txt, 2 * TXT_BLKS)
            sp.wait_ge(embed_img, 2 * IMG_BLKS)

            def loads(it, first, last):
                for u in range(2):
                    tok = it * (2 * N) + u * N
                    wait(sp, v_mm, 2 * it + u - 1)
                    wait(sp, s_mm, PER * it + PAIRS * (u - 1))
                    load(hn_b[u][:], hn[:, :, bass.ds(tok, QW)], hnb_in[u])
                    for s in range(8):
                        rows = slice(16 * s, 16 * s + 16)
                        load(q_st[u][rows], parts_dram[Q_PART[s], 0:C, bass.ds(tok, QW)]
                             .rearrange("(h d) n -> d h n", d=D), stack_in[u])
                        load(k_st[u][rows], parts_dram[K_PART[s], C:2 * C, bass.ds(tok, N)]
                             .rearrange("(h d) n -> d h n", d=D), stack_in[u])
                if first:
                    load(w_down, a["w_down"], expert_w_in)
                    load(w_up, a["w_up"], expert_w_in)

            looped(sp, loads)

            out_v = out.rearrange("(t p) c -> p t c", p=TT)
            sp.wait_ge(y_done, 1)
            sp.dma_start(out_v[:, 0:SUB, :], y_out[:]).then_inc(y_stored, 16)
            with sp.Fori(1, NBLK, 1) as i:
                sp.wait_ge(y_done, i + 1)
                sp.dma_start(out_v[:, bass.ds(i * SUB, SUB), :], y_out[:]).then_inc(y_stored, 16)
            sp.wait_ge(y_stored, 16 * NBLK)

        @block.tensor
        def _(pe):
            mm, tp = nc.tensor.matmul, nc.tensor.transpose

            pe.wait_ge(patch_in, 16 * (2 + KP))
            for i in range(IMG_BLKS):
                for m in range(2):
                    for k in range(KP):
                        last = mm(bank[2 * i + m][0:CP, 0:IMG_N], w_tok[:, k, CP * m:CP * m + CP],
                                  x_patch[:, k, IMG_N * i:IMG_N * (i + 1)], start=(k == 0), stop=(k == KP - 1))
                    last.then_inc(embed_mm, 1)
            pe.wait_ge(text_in, 16 * (1 + 4 + 32 + 3))
            pe.wait_ge(onehot_done, 1)
            for i in range(TXT_BLKS):
                for m in range(2):
                    q = 2 * i + m
                    if q >= 3:
                        pe.wait_ge(embed_txt, q - 2)
                    mm(bank[4 + q % 3][0:CP, 0:512], table[:, CP * m:CP * m + CP],
                       onehot[:, 512 * i:512 * i + 512], start=True, stop=True).then_inc(embed_mm, 1)

            def norm(base, n):
                for u in range(2):
                    if base:
                        pe.wait_ge(h_added, batches_before((n + u + 1) * BLK))
                    else:
                        pe.wait_ge(embed_img, 2 * IMG_BLKS)
                        pe.wait_ge(embed_txt, 2 * TXT_BLKS)
                    for s in range(SUB):
                        t = SUB * (n + u) + s
                        for c in range(2):
                            last = tp(bank[2 * u + s // 2][0:TT, C * (s % 2) + CP * c:][:, 0:CP],
                                      hT[:, c, TT * t:TT * t + TT], ident[0:CP, 0:CP])
                    last.then_inc(h_tp, 1)
                for u in range(2):
                    pe.wait_ge(xn_done, base + n + u + 1)
                    if base:
                        pe.wait_ge(h2_out, n + u + 1)
                    for s in range(SUB):
                        for c in range(2):
                            last = tp(bank[2 * u + c][0:CP, TT * s:TT * s + TT],
                                      xn[:, SUB * (n + u) + s, CP * c:CP * c + CP], ident[0:TT, 0:TT])
                    last.then_inc(xn_tp, 1)

            pe.wait_ge(const_in, 16 * 19)
            for n in range(0, NBLK, 2):
                norm(0, n)
                for u in range(2):
                    pe.wait_ge(hn_done, n + u + 1)
                    for t in range(3):
                        q = 3 * (n + u) + t
                        if q >= 3:
                            pe.wait_ge(rest_a, q - 2)
                        for c in range(2):
                            last = mm(bank[4 + t][:, 0:BLK], w_qk[:, c, 128 * t:128 * t + 128],
                                      hn[:, c, (n + u) * BLK:(n + u + 1) * BLK], start=(c == 0), stop=(c == 1))
                        last.then_inc(qk_mm, 1)

            def attention(it, first, last_it):
                def live(k, unit=1):
                    return (not first or k >= 0) and (not last_it or k < PER // unit)

                def scores(k):
                    h, u = 2 * (k % PAIRS), k // PAIRS % 2
                    if k % PAIRS == 0:
                        pe.wait_ge(stack_in[u], it * 256 + 256 * (k // PAIRS // 2 + 1))
                    wait(pe, exp1_b, PER * it + k)
                    for e in range(2):
                        last = mm(bank[2][64 * e:64 * e + 64, 0:N], q_st[u][:, h + e, 128:QW],
                                  k_st[u][:, h + e, :], start=True, stop=True)
                    last.then_inc(s_mm_b, 1)
                    wait(pe, exp1_a, PER * it + k - 1)
                    o = bank[k % 2]
                    mm(o[:, 0:N], q_st[u][:, h, 0:128], k_st[u][:, h, :], start=True, stop=True)
                    mm(o[:, N:N + REST], q_st[u][:, h + 1, 0:128], k_st[u][:, h + 1, 128:N], start=True, stop=True)
                    mm(o[:, N + REST:2 * N], q_st[u][:, h + 1, 0:128], k_st[u][:, h + 1, 0:128],
                       start=True, stop=True).then_inc(s_mm, 1)

                def transposes(k):
                    pe.wait_ge(att_done, PER * it + k + 1)
                    wait(pe, exp2_done, PER * it + k)
                    t = att[k % 2]
                    rest_ = t[:, AT2:AT2 + 192]
                    tp(bank[3][:, 0:128], t[:, 0:128], ident[:])
                    tp(bank[3][:, 128:128 + PW], rest_[0:PW, 0:128], ident[0:PW, 0:PW])
                    tp(bank[3][:, 128 + PW:T0W], t[:, AT1 + REST:AT1 + N], ident[:])
                    tp(bank[4][:, 64:N], rest_[0:PW, 64:192], ident[0:PW, 0:PW])
                    tp(bank[4][0:64, 128:128 + PW], rest_[0:PW, 128:192], ident[0:PW, 0:PW])
                    tp(bank[4][:, 0:128], t[:, 128:256], ident[:]).then_inc(tr_mm, 1)

                def values(g):
                    b, u = g // GROUPS, g // GROUPS % 2
                    pe.wait_ge(exp2_done, PER * it + 2 * g + 2)
                    wait(pe, o_out, PER // 2 * it + g)
                    if g % GROUPS == 0:
                        pe.wait_ge(v_out, 2 * it + b + 1)
                    p = [(2 * g + pair) % 4 for pair in range(2)]
                    parts = ([(j, slice(0, N), 0) if j % 2 == 0 else (j, slice(0, 128), 128 + PW) for j in range(4)]
                             + [(j, slice(128, N), 192) for j in (1, 3)])
                    for n, (j, dst, at) in enumerate(parts):
                        mm(bank[5][32 * j:32 * j + 32, dst], v_lo[u][:, 4 * (g % GROUPS) + j, :],
                           p_lo[p[j // 2]][:, at:at + dst.stop - dst.start], start=(n < 4), stop=False)
                    for n, (j, dst, at) in enumerate(parts):
                        last = mm(bank[5][32 * j:32 * j + 32, dst], v_hi[u][:, 4 * (g % GROUPS) + j, :],
                                  p_hi[p[j // 2]][:, dst], start=False, stop=(j % 2 == 0 or n >= 4))
                    last.then_inc(pv_mm, 1)

                def sums(g):
                    pe.wait_ge(o_out, PER // 2 * it + g + 1)
                    wait(pe, onorm_done, PER // 2 * it + g)
                    tp(bank[6][:, 0:128], o_raw[g % 2][:, 0:128], ident[:])
                    tp(bank[6][0:REST, 128:256], o_raw[g % 2][:, 128:N], ident[:]).then_inc(sum2_tp, 1)

                def sums_back(g):
                    pe.wait_ge(rep_done, PER // 2 * it + g + 1)
                    rep = rsum2_rep[:].rearrange("p c j d -> p c (j d)")
                    tp(bank[6][:, 256:384], rep[:, 0, :], ident[:])
                    tp(bank[6][:, 384:384 + REST], rep[0:REST, 1, :], ident[0:REST, 0:REST]).then_inc(rsum2_tp, 1)

                def v_proj(b):
                    u = b % 2
                    pe.wait_ge(hnb_in[u], it * 16 + 16 * (b // 2) + 16)
                    wait(pe, h_added, 2 * it + b - 1)
                    halves = w_v[:, :, :].rearrange("p c (i e d) -> p c e i d", e=2, d=D)
                    for c in range(2):
                        mm(bank[7][:, 0:C], hn_b[u][:, c, 0:128], w_v[:, c, :], start=(c == 0), stop=(c == 1))
                    for e in range(2):
                        for c in range(2):
                            last = mm(bank[7][64 * e:64 * e + 64, C:C + CP], hn_b[u][:, c, 128:QW],
                                      halves[:, c, e], start=(c == 0), stop=(c == 1))
                    last.then_inc(v_mm, 1)

                def out_proj(b):
                    pe.wait_ge(onorm_done, PER // 2 * it + GROUPS * b + GROUPS)
                    pe.wait_ge(v_out, 2 * it + (min(b + 2, 2) if last_it else b + 2))
                    for m in range(2):
                        for g in range(GROUPS):
                            last = mm(bank[7][0:CP, N * m:N * m + N], w_o[:, g, CP * m:CP * m + CP],
                                      o_norm[b % 2][:, g, :], start=(g == 0), stop=(g == GROUPS - 1))
                    last.then_inc(proj_mm, 1)

                for s in pair_steps(first, last_it):
                    if live(s + 2):
                        scores(s + 2)
                    if live(s):
                        transposes(s)
                    if s % 2 == 0 and live((s - 2) // 2, 2):
                        values((s - 2) // 2)
                    if s % 2 == 1 and live((s - 3) // 2, 2):
                        sums((s - 3) // 2)
                    if s % 2 == 0 and live((s - 4) // 2, 2):
                        sums_back((s - 4) // 2)
                    if s % PAIRS == 5 and live((s + 1) // PAIRS, PAIRS):
                        v_proj((s + 1) // PAIRS)
                    if s % PAIRS == 3 and live((s - 9) // PAIRS, PAIRS):
                        out_proj((s - 9) // PAIRS)

            looped(pe, attention)

            for n in range(0, NBLK, 2):
                norm(NBLK, n)
                for u in range(2):
                    pe.wait_ge(hn_done, NBLK + n + u + 1)
                    for c in range(2):
                        last = mm(bank[4 + u][0:CP, 0:BLK], w1[:, c, :], hn[:, c, (n + u) * BLK:(n + u + 1) * BLK],
                                  start=(c == 0), stop=(c == 1))
                    last.then_inc(g1_mm, 1)
                for u in range(2):
                    pe.wait_ge(g1_done, n + u + 1)
                    wait(pe, logit_done, n + u)
                    for s in range(SUB):
                        last = mm(bank[6][0:TT, E * s:E * s + E], g1[u][:, TT * s:TT * s + TT], w2[:],
                                  start=True, stop=True)
                    last.then_inc(logit_mm, 1)

            pe.wait_ge(expert_w_in, 32)
            pe.wait_ge(logit_done, NBLK)

            def experts(i, first):
                def down(e):
                    for half in range(2):
                        q = 2 * e + half
                        if not (first and q < 4):
                            pe.wait_ge(z_done, 2 * E * i + q - 3)
                        for c in range(2):
                            last = mm(bank[q % 4][:, 0:BLK], w_down[:, c, ED * e + 128 * half:][:, 0:128],
                                      hn[:, c, bass.ds(i * BLK, BLK)], start=(c == 0), stop=(c == 1))
                        last.then_inc(down_mm, 1)

                def up(e):
                    pe.wait_ge(z_done, 2 * E * i + 2 * e + 2)
                    if not (first and e < 2):
                        pe.wait_ge(acc_done, E * i + e - 1)
                    for s in range(SUB):
                        for half in range(2):
                            last = mm(bank[4 + 2 * (e % 2) + s // 2][0:TT, C * (s % 2):C * (s % 2) + C],
                                      z[e % 2][:, half, TT * s:TT * s + TT], w_up[:, 2 * e + half, :],
                                      start=(half == 0), stop=(half == 1))
                    last.then_inc(up_mm, 1)

                down(0)
                for e in range(E):
                    if e + 1 < E:
                        down(e + 1)
                    up(e)

            experts(0, True)
            with pe.Fori(1, NBLK, 1) as i:
                experts(i, False)

        @block.scalar
        def _(act):
            fn = nc.scalar.activation
            act.wait_ge(patch_in, 16 * (2 + KP))
            for i in range(IMG_BLKS):
                for m in range(2):
                    act.wait_ge(embed_mm, 2 * i + m + 1)
                    dst = hT[:, m, i * 8 * N:(i + 1) * 8 * N].rearrange("p (b n) -> p b n", n=N)[:, :, 0:NI]
                    fn(dst, bank[2 * i + m][0:CP, 0:IMG_N].rearrange("p (b n) -> p b n", n=NI), ACT.Identity,
                       bias=b_tok[:, m:m + 1]).then_inc(embed_img, 1)

            def norm(base, n):
                if base:
                    for u in range(2):
                        act.wait_ge(n_stat, base + n + u + 1)
                        for s in range(0, SUB, 2):
                            ins = fn(h2b[:, SUB * (n + u) + s:SUB * (n + u) + s + 2, :],
                                     bank[2 * u + s // 2][0:TT, 0:2 * C], ACT.Copy)
                        ins.then_inc(h2_out, 1)
                for u in range(2):
                    act.wait_ge(xn_tp, base + n + u + 1)
                    for c in range(2):
                        ins = fn(hn[:, c, (n + u) * BLK:(n + u + 1) * BLK], bank[2 * u + c][0:CP, 0:BLK], ACT.Copy)
                    ins.then_inc(hn_done, 1)

            act.wait_ge(const_in, 16 * 19)
            for n in range(0, NBLK, 2):
                norm(0, n)
                for u in range(2):
                    if n >= 2:
                        act.wait_ge(parts_stored[u], 24 * n)
                    for t in range(3):
                        q = 3 * (n + u) + t
                        act.wait_ge(qk_mm, q + 1)
                        fn(part[u][:, t, :], bank[4 + t][:, 0:BLK], ACT.Copy,
                           scale=qk_scale[:, t:t + 1]).then_inc(part_a, 1)
                        act.wait_ge(rest_a, q + 1)
                        fn(part[u][:, 3 + t, :], rest[u][:, t, :], ACT.Copy).then_inc(part_b, 1)

            def attention(it, first, last_it):
                def live(k, unit=1):
                    return (not first or k >= 0) and (not last_it or k < PER // unit)

                def exp1(k, units):
                    src = [bank[k % 2][:, 0:N], bank[k % 2][:, N:2 * N], bank[2][:, 0:N]]
                    for w in units:
                        ins = fn(e1[k % 2][:, w, :], src[w], ACT.Exp, bias=neg_max[k % 2][:, w:w + 1],
                                 accum_out=sum1[k % 2][:, w:w + 1])
                    return ins

                def exp2(k):
                    act.wait_ge(tr_mm, PER * it + k + 1)
                    wait(act, pv_mm, PER // 2 * it + k // 2 - 1)
                    fn(p_lo[k % 4][:], bank[3][:, 0:T0W], ACT.Exp)
                    fn(p_hi[k % 4][:], bank[4][:, 0:N], ACT.Exp).then_inc(exp2_done, 1)

                def out_raw(g):
                    act.wait_ge(pv_mm, PER // 2 * it + g + 1)
                    wait(act, onorm_done, PER // 2 * it + g - 1)
                    fn(o_raw[g % 2][:], bank[5][:, 0:N], ACT.Copy).then_inc(o_out, 1)

                def v_copy(b):
                    act.wait_ge(v_mm, 2 * it + b + 1)
                    fn(v_lo[b % 2][:, :, 0:D], bank[7][:, 0:C].rearrange("p (h d) -> p h d", d=D), ACT.Copy)
                    for e in range(2):
                        rows = slice(64 * e, 64 * e + REST)
                        ins = fn(v_hi[b % 2][rows, e::2, 0:D],
                                 bank[7][rows, C:C + CP].rearrange("p (h d) -> p h d", d=D), ACT.Copy)
                    ins.then_inc(v_out, 1)

                for s in pair_steps(first, last_it):
                    if s % 2 == 1 and live((s - 3) // 2, 2):
                        out_raw((s - 3) // 2)
                    if s % PAIRS == 0 and live(s // PAIRS, PAIRS):
                        v_copy(s // PAIRS)
                    if live(s + 2):
                        act.wait_ge(max_b, PER * it + s + 3)
                        exp1(s + 2, (2,)).then_inc(exp1_b, 1)
                    if live(s):
                        exp2(s)
                    if live(s + 2):
                        act.wait_ge(max_done, PER * it + s + 3)
                        exp1(s + 2, (0, 1)).then_inc(exp1_a, 1)

            looped(act, attention)

            for u in range(2):
                act.wait_ge(hnb_in[u], 16 * B // 2)
            for n in range(0, NBLK, 2):
                norm(NBLK, n)
                for u in range(2):
                    act.wait_ge(g1_mm, n + u + 1)
                    fn(g1[u][:], bank[4 + u][0:CP, 0:BLK], ACT.Gelu, bias=b1[:]).then_inc(g1_done, 1)
            act.wait_ge(route_dve, 1)
            fn(expl[:], shifted[:], ACT.Exp).then_inc(route_exp, 1)

            act.wait_ge(fin_dve, 5)

            def experts(i, first):
                for e in range(E):
                    for half in range(2):
                        act.wait_ge(down_mm, 2 * E * i + 2 * e + half + 1)
                        if half == 0 and not (first and e < 2):
                            act.wait_ge(up_mm, E * i + e - 1)
                        fn(z[e % 2][:, half, :], bank[(2 * e + half) % 4][:, 0:BLK], ACT.Gelu,
                           bias=down_b[:, 2 * e + half:2 * e + half + 1]).then_inc(z_done, 1)

            experts(0, True)
            with act.Fori(1, NBLK, 1) as i:
                experts(i, False)

        @block.vector
        def _(dve):
            v = nc.vector
            v.memset(hn[:, :, T:TPAD], 0.0)
            v.memset(one[:], 1.0)
            for u in range(2):
                v.memset(v_lo[u][:], 1.0)
                v.memset(v_hi[u][:], 0.0)
                v.memset(att[u][:], 0.0)
            v.memset(bank[6][:], 1.0).then_inc(zeroed, 1)
            dve.wait_ge(zeroed, 1)
            for u in range(2):
                for e in range(2):
                    v.memset(v_hi[u][64 * e:64 * e + REST, e::2, D:2 * D], 1.0)
            v.memset(zero[:], 0.0).then_inc(preset, 1)

            dve.wait_ge(text_in, 16 * (1 + 4 + 32 + 3))
            v.tensor_scalar(onehot, tok_i, float(VOC - 1), iota[:, 0:1], ALU.min, ALU.is_equal)\
                .then_inc(onehot_done, 1)
            for i in range(TXT_BLKS):
                for m in range(2):
                    q = 2 * i + m
                    dve.wait_ge(embed_mm, 2 * IMG_BLKS + q + 1)
                    dst = hT[:, m, i * TXT_B * N:(i + 1) * TXT_B * N].rearrange("p (b n) -> p b n", n=N)[:, :, NI:N]
                    v.scalar_tensor_tensor(
                        out=dst, in0=bank[4 + q % 3][0:CP, :].rearrange("p (b n) -> p b n", n=NT),
                        scalar=float(C) ** 0.5, in1=pe_sb[:, m, :].unsqueeze(1).to_broadcast([CP, TXT_B, NT]),
                        op0=ALU.mult, op1=ALU.add).then_inc(embed_txt, 1)

            def norm(base, n):
                for u in range(2):
                    k = base + n + u + 1
                    t0 = SUB * (n + u)
                    dve.wait_ge(h_tp, k)
                    for s in range(SUB):
                        ins = v.bn_stats(n_stats[:, t0 + s, :],
                                         bank[2 * u + s // 2][0:TT, C * (s % 2):C * (s % 2) + C])
                    ins.then_inc(n_stat, 1)
                    dve.wait_ge(n_stat, k)
                    for s in range(SUB):
                        ins = v.bn_aggr(n_mv[:, t0 + s, :], n_stats[:, t0 + s, :])
                    ins.then_inc(n_mv_done, 1)
                for u in range(2):
                    k = base + n + u + 1
                    dve.wait_ge(n_rstd_done, k)
                    if base:
                        dve.wait_ge(h2_out, n + u + 1)
                    for s in range(SUB):
                        t = SUB * (n + u) + s
                        ins = v.tensor_scalar(xn[:, t, :], bank[2 * u + s // 2][0:TT, C * (s % 2):C * (s % 2) + C],
                                              n_mv[:, t, 0:1], n_rstd[:, t:t + 1], ALU.subtract, ALU.mult)
                    ins.then_inc(xn_done, 1)

            dve.wait_ge(const_in, 16 * 19)
            dve.wait_ge(embed_img, 2 * IMG_BLKS)
            dve.wait_ge(embed_txt, 2 * TXT_BLKS)

            def split(n):
                for t in range(3):
                    dve.wait_ge(part_a, 3 * n + t + 1)
                    if n >= 2 and t == 0:
                        dve.wait_ge(part_c, 3 * (n - 1))
                    v.scalar_tensor_tensor(
                        out=rest[n % 2][:, t, :], in0=bank[4 + t][:, 0:BLK], scalar=qk_scale[:, t:t + 1],
                        in1=part[n % 2][:, t, :], op0=ALU.mult, op1=ALU.subtract).then_inc(rest_a, 1)

            for n in range(0, NBLK, 2):
                norm(0, n)
                split(n)
                split(n + 1)

            def attention(it, first, last_it):
                def live(k, unit=1):
                    return (not first or k >= 0) and (not last_it or k < PER // unit)

                def maxima(k):
                    dve.wait_ge(s_mm_b, PER * it + k + 1)
                    v.tensor_reduce(neg_max[k % 2][:, 2:3], bank[2][:, 0:N], AX_X, ALU.max, negate=True)\
                        .then_inc(max_b, 1)
                    dve.wait_ge(s_mm, PER * it + k + 1)
                    v.tensor_reduce(neg_max[k % 2][:, 0:2], bank[k % 2][:, 0:2 * N].rearrange("p (e n) -> p e n", e=2),
                                    AX_X, ALU.max, negate=True).then_inc(max_done, 1)

                def normalise(k):
                    dve.wait_ge(exp1_a, PER * it + k + 1)
                    v.reciprocal(rsum1[k % 2][:], sum1[k % 2][:]).then_inc(rsum_done, 1)
                    wait(dve, tr_mm, PER * it + k - 1)
                    dve.wait_ge(rsum_done, PER * it + k + 1)
                    for w, (at, mask) in enumerate(((0, mask_a), (AT1, mask_r), (AT2, mask_b))):
                        ins = v.scalar_tensor_tensor(
                            out=att[k % 2][:, at:at + N], in0=e1[k % 2][:, w, :],
                            scalar=rsum1[k % 2][:, w:w + 1], in1=mask[:], op0=ALU.mult, op1=ALU.mult)
                    ins.then_inc(att_done, 1)

                def reciprocals(g):
                    dve.wait_ge(sum2_tp, PER // 2 * it + g + 1)
                    wait(dve, rep_done, PER // 2 * it + g)
                    sums = bank[6][:, 0:256].rearrange("p (c j d) -> p c j d", c=2, j=4)[:, :, :, D]
                    v.reciprocal(rsum2[:], sums).then_inc(rsum2_done, 1)

                def scale_out(g):
                    dve.wait_ge(rsum2_tp, PER // 2 * it + g + 1)
                    v.tensor_tensor(o_norm[g // GROUPS % 2][:, g % GROUPS, :], o_raw[g % 2][:],
                                    bank[6][:, 256:256 + N], ALU.mult).then_inc(onorm_done, 1)

                def add_out(b):
                    dve.wait_ge(proj_mm, 2 * it + b + 1)
                    for m in range(2):
                        h = hT[:, m, bass.ds(it * (2 * N) + b * N, N)]
                        ins = v.scalar_tensor_tensor(out=h, in0=bank[7][0:CP, N * m:N * m + N],
                                                     scalar=b_o[:, m:m + 1], in1=h, op0=ALU.add, op1=ALU.add)
                    ins.then_inc(h_added, 1)

                for s in pair_steps(first, last_it):
                    if s % 2 == 1 and live((s - 5) // 2, 2):
                        scale_out((s - 5) // 2)
                    if s % 2 == 0 and live((s - 4) // 2, 2):
                        reciprocals((s - 4) // 2)
                    if s % PAIRS == 4 and live((s - 10) // PAIRS, PAIRS):
                        add_out((s - 10) // PAIRS)
                    if live(s + 2):
                        maxima(s + 2)
                    if live(s + 1):
                        normalise(s + 1)

            looped(dve, attention)

            def logits(n):
                dve.wait_ge(logit_mm, n + 1)
                v.tensor_tensor(logit[:, SUB * n:SUB * n + SUB, :],
                                bank[6][0:TT, 0:SUB * E].rearrange("p (s e) -> p s e", e=E),
                                b2[:].unsqueeze(1).to_broadcast([TT, SUB, E]), ALU.add).then_inc(logit_done, 1)

            for n in range(0, NBLK, 2):
                norm(NBLK, n)
                logits(n)
                logits(n + 1)
            dve.wait_ge(logit_done, NBLK)
            of_e = logit[:].unsqueeze(3).to_broadcast([TT, NTILE, E, E])
            of_j = logit[:].unsqueeze(2).to_broadcast([TT, NTILE, E, E])
            flat = [TT, NTILE, E * E]
            v.tensor_reduce(top[:], logit[:], AX_X, ALU.max).then_inc(fin_dve, 1)
            v.tensor_tensor(cmp_ge, of_j, of_e, ALU.is_ge).then_inc(fin_dve, 1)
            v.tensor_tensor(cmp_gt[:], of_j, of_e, ALU.is_gt).then_inc(fin_dve, 1)
            dve.wait_ge(fin_dve, 1)
            v.tensor_tensor(shifted[:], logit[:], top[:].unsqueeze(2).to_broadcast([TT, NTILE, E]),
                            ALU.subtract).then_inc(route_dve, 1)
            dve.wait_ge(fin_dve, 3)
            ge, gt = (t.rearrange("p t e j -> p t (e j)") for t in (cmp_ge, cmp_gt[:]))
            tri = earlier[:].rearrange("p e j -> p (e j)").unsqueeze(1).to_broadcast(flat)
            v.tensor_tensor(ge, ge, tri, ALU.mult).then_inc(fin_dve, 1)
            dve.wait_ge(fin_dve, 4)
            v.tensor_tensor(gt, gt, ge, ALU.max).then_inc(fin_dve, 1)
            dve.wait_ge(fin_dve, 5)
            v.tensor_reduce(rank[:], cmp_gt[:], AX_X, ALU.add).then_inc(fin_dve, 1)
            dve.wait_ge(fin_dve, 6)
            dve.wait_ge(route_exp, 1)
            v.scalar_tensor_tensor(out=kept[:].rearrange("p t e -> p (t e)"), in0=rank[:].rearrange("p t e -> p (t e)"),
                                   scalar=1.5, in1=expl[:].rearrange("p t e -> p (t e)"),
                                   op0=ALU.is_lt, op1=ALU.mult).then_inc(fin_dve, 1)
            v.tensor_reduce(sum_e[:], expl[:], AX_X, ALU.add).then_inc(fin_dve, 1)
            dve.wait_ge(fin_dve, 7)
            v.tensor_reduce(sum_k[:], kept[:], AX_X, ALU.add).then_inc(fin_dve, 1)
            dve.wait_ge(fin_dve, 9)
            v.scalar_tensor_tensor(out=sum_k[:], in0=sum_e[:], scalar=GATE_EPS, in1=sum_k[:],
                                   op0=ALU.mult, op1=ALU.add).then_inc(fin_dve, 1)
            dve.wait_ge(fin_dve, 10)
            v.reciprocal(sum_e[:], sum_k[:]).then_inc(fin_dve, 1)
            dve.wait_ge(fin_dve, 11)
            v.tensor_tensor(gate[:], kept[:], sum_e[:].unsqueeze(2).to_broadcast([TT, NTILE, E]),
                            ALU.mult).then_inc(fin_dve, 1)
            dve.wait_ge(fin_dve, 12)

            def experts(i, first):
                v.tensor_copy(gate_b[:], gate[:, bass.ds(i * SUB, SUB), :]).then_inc(gate_cp, 1)
                wait(dve, y_done, i)
                dve.wait_ge(gate_cp, i + 1)
                for e in range(E):
                    dve.wait_ge(up_mm, E * i + e + 1)
                    wait(dve, acc_done, E * i + e)
                    for s in range(SUB):
                        before = acc[:, s, :] if e else xn[:, bass.ds(i * SUB + s, 1), :].squeeze(1)
                        ins = v.scalar_tensor_tensor(
                            out=acc[:, s, :], in0=bank[4 + 2 * (e % 2) + s // 2][0:TT, C * (s % 2):C * (s % 2) + C],
                            scalar=gate_b[:, s, e:e + 1], in1=before, op0=ALU.mult, op1=ALU.add)
                    ins.then_inc(acc_done, 1)
                dve.wait_ge(acc_done, E * i + E)
                for s in range(SUB):
                    ins = v.bn_stats(stats[:, s, :], acc[:, s, :])
                ins.then_inc(fin_dve, 1)
                dve.wait_ge(fin_dve, 13 + 3 * i)
                dve.sem_inc(stats_seen, 1)
                for s in range(SUB):
                    ins = v.bn_aggr(mv[:, s, :], stats[:, s, :])
                ins.then_inc(mv_done, 1)
                dve.wait_ge(rstdy_done, i + 1)
                dve.wait_ge(mv_done, i + 1)
                for s in range(SUB):
                    ins = v.tensor_scalar(acc[:, s, :], acc[:, s, :], mv[:, s, 0:1], rstd_y[:, s:s + 1],
                                          ALU.subtract, ALU.mult)
                ins.then_inc(fin_dve, 1)
                dve.wait_ge(fin_dve, 14 + 3 * i)
                v.tensor_tensor(acc, acc, gamma[:].unsqueeze(1).to_broadcast([TT, SUB, C]), ALU.mult)\
                    .then_inc(fin_dve, 1)
                dve.wait_ge(fin_dve, 15 + 3 * i)
                dve.wait_ge(h2b_done, 1)
                wait(dve, y_stored, 16 * i)
                v.tensor_tensor(y_out[:], acc, h2b[:, bass.ds(i * SUB, SUB), :], ALU.add).then_inc(y_done, 1)

            experts(0, True)
            with dve.Fori(1, NBLK, 1) as i:
                experts(i, False)

        @block.gpsimd
        def _(pool):
            g = nc.gpsimd

            def norm(base, n):
                for u in range(2):
                    k = base + n + u + 1
                    t = slice(SUB * (n + u), SUB * (n + u + 1))
                    pool.wait_ge(n_mv_done, k)
                    g.tensor_tensor(n_var[:, t], n_mv[:, t, 1], eps[:].to_broadcast([TT, SUB]), ALU.add)\
                        .then_inc(n_var_done, 1)
                    pool.wait_ge(n_var_done, k)
                    g.tensor_tensor(n_rstd[:, t], n_var[:, t], neg_half[0:TT, :].to_broadcast([TT, SUB]), ALU.pow)\
                        .then_inc(n_rstd_done, 1)

            pool.wait_ge(preset, 1)
            pool.wait_ge(const_in, 16 * 19)
            for n in range(0, NBLK, 2):
                norm(0, n)
                for u in range(2):
                    for t in range(3):
                        pool.wait_ge(part_b, 3 * (n + u) + t + 1)
                        g.tensor_tensor(part[u][:, 6 + t, :], rest[u][:, t, :], part[u][:, 3 + t, :],
                                        ALU.subtract).then_inc(part_c, 1)

            def attention(it, first, last_it):
                for j in range(PER // 2):
                    pool.wait_ge(rsum2_done, PER // 2 * it + j + 1)
                    wait(pool, rsum2_tp, PER // 2 * it + j)
                    g.tensor_tensor(rsum2_rep[:].rearrange("p c j d -> p (c j) d"),
                                    rsum2[:].rearrange("p c j -> p (c j)").unsqueeze(2).to_broadcast([128, 8, 2 * D]),
                                    one[:].unsqueeze(2).to_broadcast([128, 8, 2 * D]), ALU.mult)\
                        .then_inc(rep_done, 1)

            looped(pool, attention)
            for n in range(0, NBLK, 2):
                norm(NBLK, n)

            pool.wait_ge(h2_out, NBLK)
            g.tensor_tensor(h2b, h2b, beta[:].unsqueeze(1).to_broadcast([TT, NTILE, C]), ALU.add)\
                .then_inc(h2b_done, 1)

            def experts(i, first):
                pool.wait_ge(mv_done, i + 1)
                g.tensor_tensor(vy[:], mv[:, :, 1], eps[:].to_broadcast([TT, SUB]), ALU.add).then_inc(vy_done, 1)
                pool.wait_ge(vy_done, i + 1)
                g.tensor_tensor(rstd_y[:], vy[:], neg_half[0:TT, :].to_broadcast([TT, SUB]), ALU.pow)\
                    .then_inc(rstdy_done, 1)

            experts(0, True)
            with pool.Fori(1, NBLK, 1) as i:
                experts(i, False)


def constants():
    f = np.float32
    q = np.arange(128)
    k = np.arange(N)
    def mask(rows):
        return np.where((rows % NUM)[:, None] == (k % NUM)[None, :], f(0.5), f(1.0)).astype(f)
    pos = np.arange(NT, dtype=f)[:, None]
    inv = np.exp(-(np.arange(0, C, 2, dtype=f) / f(C)) * f(np.log(10000.0))).astype(f)
    ang = (pos * inv).astype(f)
    pe = np.stack([np.sin(ang), np.cos(ang)], axis=-1).reshape(NT, C).astype(f)
    scale = np.where(np.arange(2 * C) < C, f(D) ** f(-0.5), f(1.0)).astype(f)
    e = np.arange(E)
    return {
        "iota": np.arange(VOC, dtype=f)[:, None],
        "pe": pe.T.reshape(2, CP, NT).transpose(1, 0, 2),
        "eps": np.full((TT, 1), LN_EPS, f),
        "neg_half": np.full((128, 1), -0.5, f),
        "qk_scale": scale.reshape(3, 128).T,
        "ident": np.eye(128, dtype=f),
        "mask_a": mask(q),
        "mask_b": mask(128 + q % 64),
        "mask_r": np.roll(mask(q), REST, axis=1),
        "earlier": np.broadcast_to((e[None, :] < e[:, None]).astype(f), (TT, E, E)),
    }


def kernel(**inputs):
    import concourse.bacc as bacc
    from concourse.bass_utils import run_bass_kernel_spmd

    i = {k: np.asarray(v) for k, v in inputs.items()}

    def chunks(w):
        return w.reshape(2, CP, -1).transpose(1, 0, 2)

    w_o = np.zeros((4, 32, GROUPS, C), np.float32)
    w_o[:, :D] = i["L0_attn_w_out"].T.reshape(GROUPS, 4, D, C).transpose(1, 2, 0, 3)
    arrays = {
        "x_patch": i["x"].reshape(B, 3, 7, 2, 8, 7, 16).transpose(4, 6, 1, 3, 0, 2, 5).reshape(128, KP, NPATCH),
        "w_tok": i["L0_tok_W"].reshape(C, 2, 8, 16, 3).transpose(2, 3, 4, 1, 0).reshape(128, KP, C),
        "b_tok": i["L0_tok_b"].reshape(2, CP).T,
        "tokens": i["x_txt"].reshape(B * NT),
        "color": i["L0_txt_color_W"], "shape": i["L0_txt_shape_W"],
        "quantity": i["L0_txt_quantity_W"], "special": i["L0_txt_special_W"],
        "w_qk": chunks(i["L0_attn_w_qkv"][:2 * C].T), "w_v": chunks(i["L0_attn_w_qkv"][2 * C:].T),
        "w_o": w_o.reshape(128, GROUPS, C), "b_o": i["L0_attn_b_out"].reshape(2, CP).T,
        "w1": chunks(i["L0_ffn_w1"]), "b1": i["L0_ffn_b1"].reshape(CP, 1),
        "w2": i["L0_ffn_w2"], "b2": i["L0_ffn_b2"],
        "w_down": i["L0_ffn_down_w"].reshape(E, 2, CP, ED).transpose(2, 1, 0, 3).reshape(CP, 2, E * ED),
        "down_b": i["L0_ffn_down_b"].reshape(2 * E, 128).T,
        "w_up": i["L0_ffn_up_w"].reshape(2 * E, 128, C).transpose(1, 0, 2),
        "gamma": i["L0_ffn_gamma"], "beta": i["L0_ffn_beta"],
        **constants(),
    }
    arrays = {k: np.ascontiguousarray(v) for k, v in arrays.items()}
    nc = bacc.Bacc("TRN2", target_bir_lowering=False, num_devices=1)
    aps = {k: nc.dram_tensor(f"in_{k}", v.shape, mybir.dt.from_np(v.dtype), kind="ExternalInput").ap()
           for k, v in arrays.items()}
    out = nc.dram_tensor("out", (T, C), F32, kind="ExternalOutput").ap()
    build(nc, aps, out)
    r = run_bass_kernel_spmd(nc, [{f"in_{k}": v for k, v in arrays.items()}], core_ids=[0])
    return r.results[0]["out"].reshape(B, N, C)
```

```python
from contextlib import ExitStack

import numpy as np

import concourse.bass as bass
from concourse import mybir

F32 = mybir.dt.float32
BF16 = mybir.dt.bfloat16
F32R = mybir.dt.float32r
I32 = mybir.dt.int32
ALU = mybir.AluOpType
ACT = mybir.ActivationFunctionType
AX_X = mybir.AxisListType.X

B = 16
NI, NT = 49, 128
N = NI + NT
T = B * N
C = 192
CP = C // 2
H, D = 12, 16
NUM = N // 4
KP = 6
NPATCH = B * NI
VOC = 70
E, ED = 8, 256
LN_EPS = 1e-5
GATE_EPS = 1e-8

BLK = 472
NBLK = T // BLK
TT = 118
SUB = BLK // TT
TPAD = T + 16

QW = 192
REST = N - 128
PW = 64 + REST
UNITS = 3
PAIRS = H // 2
NPAIR = B * PAIRS
PER = 2 * PAIRS
NIT = NPAIR // PER
GROUPS = PAIRS // 2
T0W = 128 + PW + 128
AT1 = 192
AT2 = AT1 + N
ATW = AT2 + 192
NTILE = NBLK * SUB
F0, F1 = 128, C - 128
WCHUNK = 256
DRAIN = 5

Q_PART = [0, 0, 0, 1, 1, 1, 2, 2]
K_PART = [0, 1, 2, 0, 1, 2, 0, 1]


EARLY = (("ident", (128, 128)), ("w_qk", (CP, 2, 2 * C)), ("qk_scale", (128, 3)),
         ("neg_half", (128, 1)), ("eps", (TT, 1)))
LATE = (("mask_a", (128, N)), ("mask_r", (128, N)), ("mask_b", (128, N)), ("w_v", (CP, 2, C)),
        ("w_o", (128, GROUPS, C)), ("b_o", (CP, 2)), ("b1", (CP, 1)), ("w2", (CP, E)),
        ("earlier", (TT, E, E)), ("later", (TT, E)), ("down_b", (128, 2 * E)))


def words(shape):
    return int(np.prod(shape[1:]))


def wait(eng, sem, value):
    if not (isinstance(value, int) and value <= 0):
        eng.wait_ge(sem, value)


def pair_steps(first, last):
    return range(-2 if first else 0, PER + (DRAIN if last else 0))


def looped(eng, body):
    body(0, True, False)
    with eng.Fori(1, NIT - 1, 1) as it:
        body(it, False, False)
    body(NIT - 1, False, True)


def build(nc, a, out):
    with ExitStack() as ctx:
        def sb(name, shape, dt=F32, phase=ctx):
            return phase.enter_context(nc.sbuf_tensor(name, shape, dt))

        def sem(name):
            return ctx.enter_context(nc.semaphore(name))

        bank = [ctx.enter_context(nc.psum_tensor(f"bank{i}", [128, 512], F32)) for i in range(8)]
        parts_dram = nc.dram_tensor("qk_parts", (3, 2 * C, TPAD), BF16).ap()

        hT = sb("hT", [CP, 2, T])
        b_tok = sb("b_tok", [CP, 2])
        table = sb("table", [VOC, C])
        iota = sb("iota", [VOC, 1])
        pe_sb = sb("pe_sb", [CP, 2, NT])
        one = sb("one", [128, 1])
        early = sb("early", [128, sum(words(s) for _, s in EARLY)])
        late = sb("late", [128, sum(words(s) for _, s in LATE)])
        w1_hi = sb("w1_hi", [128, CP], F32R)
        w1_lo = sb("w1_lo", [128, CP], F32R)
        w1_1 = sb("w1_1", [128, CP], F32R)
        b2 = sb("b2", [TT, E])
        gamma = sb("gamma", [TT, C])
        beta = sb("beta", [TT, C])
        zero = sb("zero", [128, 16], BF16)

        area_c = sb("area_c", [128, 7264])
        with ExitStack() as until_attention:
            area_b, area_h, area_a, area_d = (
                sb(name, [128, size], phase=until_attention) for name, size in
                (("area_b", 9216), ("area_h", 2 * TPAD), ("area_a", 8960), ("area_d", 5440)))
        wd_hi, wd_lo, wd_1 = (sb(name, [128, E * ED], F32R) for name in ("wd_hi", "wd_lo", "wd_1"))
        w_up = sb("w_up", [128, 2 * E, C])
        x_hi, x_lo, x1_hi, x1_lo = (sb(name, [128, T], F32R) for name in ("x_hi", "x_lo", "x1_hi", "x1_lo"))
        area_e = sb("area_e", [128, 9216 + 2 * TPAD + 8960 + 5440 - 9216 - 4 * T])

        def carve(area, at, shape, dt=F32):
            n = int(np.prod(shape[1:]))
            size = n if dt is not BF16 else n // 2
            v = area[0:shape[0], at:at + size]
            if dt is not F32:
                v = v.bitcast(dt)
            names = ["x", "y", "z"][:len(shape) - 1]
            if len(names) > 1:
                v = v.rearrange(f"p ({' '.join(names)}) -> p {' '.join(names)}",
                                **dict(zip(names[1:], shape[2:])))
            return v, at + size

        packed = {}
        for area, fields in ((early, EARLY), (late, LATE)):
            o = 0
            for name, shape in fields:
                packed[name], o = carve(area, o, list(shape))
        (ident, w_qk, qk_scale, neg_half, eps, mask_a, mask_r, mask_b, w_v, w_o, b_o, b1, w2, earlier, later,
         down_b) = (packed[name] for name, _ in EARLY + LATE)
        hn, o = carve(area_h, 0, [CP, 2, TPAD])

        x_patch, o = carve(area_a, 0, [128, KP, NPATCH])
        tok_i, o = carve(area_a, o, [VOC, B * NT], I32)
        onehot, o = carve(area_a, o, [VOC, B * NT])
        q_st, k_st, o = [None] * 2, [None] * 2, 0
        for u in range(2):
            q_st[u], o = carve(area_a, o, [128, H, QW], BF16)
            k_st[u], o = carve(area_a, o, [128, H, N], BF16)
        part, o = [None] * 2, 0
        rest = [None] * 2
        for u in range(2):
            part[u], o = carve(area_b, o, [128, 9, BLK], BF16)
            rest[u], o = carve(area_b, o, [128, 3, BLK])
        wd_raw, o = carve(area_c, 0, [128, E * ED])
        wd_1_raw, o = carve(area_c, o, [128, E * ED])
        w1_raw, o = carve(area_c, o, [128, CP])
        w1_1_raw, o = carve(area_c, o, [128, CP])
        h2b, o = carve(area_e, 0, [TT, NTILE, C])
        cmp_ge, o = carve(area_e, o, [TT, NTILE, E, E])
        o -= NTILE * E * E
        z = [None] * 2
        for u in range(2):
            z[u], o = carve(area_e, o, [128, 2, BLK])
        xn, o = carve(area_c, 0, [TT, NTILE, C])
        w_tok, _ = carve(area_c, o, [128, KP, C])
        acc, o = carve(area_c, o, [TT, SUB, C])
        y_out = sb("y_out", [TT, SUB, C])
        n_stats = sb("n_stats", [TT, NTILE, 6])
        n_mv = sb("n_mv", [TT, NTILE, 2])
        n_var = sb("n_var", [TT, NTILE])
        n_rstd = sb("n_rstd", [TT, NTILE])

        hn_b = [sb(f"hn_b{u}", [CP, 2, QW]) for u in range(2)]
        v_lo = [sb(f"v_lo{u}", [128, H, 2 * D]) for u in range(2)]
        v_hi = [sb(f"v_hi{u}", [128, H, 2 * D]) for u in range(2)]
        neg_max = [sb(f"neg_max{u}", [128, UNITS]) for u in range(2)]
        e1, att, p_lo, p_hi, o_norm, o = [None] * 2, [None] * 2, [None] * 4, [None] * 4, [None] * 2, 0
        for u in range(2):
            e1[u], o = carve(area_d, o, [128, UNITS, N])
            att[u], o = carve(area_d, o, [128, ATW])
            o_norm[u], o = carve(area_d, o, [128, GROUPS, N])
        for u in range(4):
            p_lo[u], o = carve(area_d, o, [128, T0W])
            p_hi[u], o = carve(area_d, o, [128, N])
        sum1 = [sb(f"sum1_{u}", [128, UNITS]) for u in range(2)]
        rsum1 = [sb(f"rsum1_{u}", [128, UNITS]) for u in range(2)]
        o_raw = [sb(f"o_raw{u}", [128, N]) for u in range(2)]
        rsum2 = sb("rsum2", [128, 2, 4])
        rsum2_rep = sb("rsum2_rep", [128, 2, 4, 2 * D])

        g1 = [sb(f"g1_{u}", [CP, BLK]) for u in range(2)]
        logit = sb("logit", [TT, NBLK * SUB, E])
        top = sb("top", [TT, NTILE])
        rank = sb("rank", [TT, NTILE, E])
        behind = sb("behind", [TT, NTILE, E])
        shifted = sb("shifted", [TT, NTILE, E])
        expl = sb("expl", [TT, NTILE, E])
        kept = sb("kept", [TT, NTILE, E])
        sum_k = sb("sum_k", [TT, NTILE])
        sum_e = sb("sum_e", [TT, NTILE])
        gate = sb("gate", [TT, NTILE, E])
        gate_b = sb("gate_b", [TT, SUB, E])
        stats = sb("stats", [TT, SUB, 6])
        mv = sb("mv", [TT, SUB, 2])
        rstd_y = sb("rstd_y", [TT, SUB])
        vy = sb("vy", [TT, SUB])

        patch_in = [sem(f"patch_in{i}") for i in range(2)]
        text_in, early_in, late_in = (sem(n) for n in ("text_in", "early_in", "late_in"))
        w_hi_done, w_lo_done = sem("w_hi_done"), sem("w_lo_done")
        x_lo_done = sem("x_lo_done")
        compared, ahead_done, rank_done = (sem(n) for n in ("compared", "ahead_done", "rank_done"))
        expert_w_in = sem("expert_w_in")
        preset = sem("preset")
        zeroed = sem("zeroed")
        onehot_done, embed_mm, embed_img, embed_txt = (sem(n) for n in
            ("onehot_done", "embed_mm", "embed_img", "embed_txt"))
        h_tp, n_stat, n_mv_done, n_var_done, n_rstd_done, xn_done, xn_tp, hn_done, h2_out, h2b_done = (
            sem(n) for n in ("h_tp", "n_stat", "n_mv_done", "n_var_done", "n_rstd_done", "xn_done", "xn_tp",
                             "hn_done", "h2_out", "h2b_done"))
        qk_mm, part_a, rest_a, part_b, part_c, pad_stored = (sem(n) for n in
            ("qk_mm", "part_a", "rest_a", "part_b", "part_c", "pad_stored"))
        parts_stored = [sem(f"parts_stored{u}") for u in range(2)]
        hnb_in = [sem(f"hnb_in{u}") for u in range(2)]
        stack_in = [sem(f"stack_in{u}") for u in range(2)]
        s_mm_b, s_mm, max_b, max_done, exp1_b, exp1_a, rsum_done, att_done, tr_mm, exp2_done, pv_mm = (sem(n) for n in
            ("s_mm_b", "s_mm", "max_b", "max_done", "exp1_b", "exp1_a", "rsum_done", "att_done", "tr_mm", "exp2_done", "pv_mm"))
        v_mm, v_out, o_out, sum2_tp, rsum2_done, rep_done, rsum2_tp, onorm_done, proj_mm, h_added = (sem(n) for n in
            ("v_mm", "v_out", "o_out", "sum2_tp", "rsum2_done", "rep_done", "rsum2_tp", "onorm_done", "proj_mm", "h_added"))
        g1_mm, g1_done, logit_mm, logit_done, route_dve, route_exp = (sem(n) for n in
            ("g1_mm", "g1_done", "logit_mm", "logit_done", "route_dve", "route_exp"))
        down_mm, z_done, up_mm, acc_done = (sem(n) for n in
            ("down_mm", "z_done", "up_mm", "acc_done"))
        gate_cp, fin_dve, stats_seen, mv_done, vy_done, rstdy_done, y_done, y_stored = (sem(n) for n in
            ("gate_cp", "fin_dve", "stats_seen", "mv_done", "vy_done", "rstdy_done", "y_done", "y_stored"))

        block = ctx.enter_context(nc.Block())
        TXT_BANK = (4, 5, 7)
        NWCHUNK = E * ED // WCHUNK
        IMG_BLKS, IMG_N = 2, NPATCH // 2
        TXT_BLKS, TXT_B = 4, 4

        def batches_before(tokens):
            return -(-tokens // N)

        def blk(t, n, width=BLK):
            return t[:, :, bass.ds(n * BLK, width)]

        TEXT_DMAS = 1 + 1 + 4 * (1 + 4 + 1) + 2
        LATE_DMAS = 4

        @block.sync
        def _(sp):
            def load(dst, src, s):
                sp.dma_start(dst, src).then_inc(s, 16)

            load(w_tok, a["w_tok"], patch_in[0])
            load(b_tok[:], a["b_tok"], patch_in[0])
            for i in range(IMG_BLKS):
                cols = slice(IMG_N * i, IMG_N * (i + 1))
                load(x_patch[:, :, cols], a["x_patch"][:, :, cols], patch_in[i])
            load(tok_i, a["tokens"].partition_broadcast(VOC), text_in)
            load(iota[:], a["iota"], text_in)
            for i in range(4):
                load(table[16 * i:16 * i + 16, 0:64], a["color"][i, :].partition_broadcast(16), text_in)
                for j in range(4):
                    load(table[16 * j + i:16 * j + 16:4, 64:128], a["shape"], text_in)
                load(table[i:64:4, 128:C], a["quantity"][i, :].partition_broadcast(16), text_in)
            load(table[64:VOC, :], a["special"], text_in)
            load(pe_sb[:], a["pe"], text_in)
            load(early[:], a["early"], early_in)
            load(late[:], a["late"], late_in)
            load(b2[:], a["b2"].partition_broadcast(TT), late_in)
            load(gamma[:], a["gamma"].partition_broadcast(TT), late_in)
            load(beta[:], a["beta"].partition_broadcast(TT), late_in)

            sp.wait_ge(preset, 1)
            for t in range(9):
                load(parts_dram[t // 3, 128 * (t % 3):128 * (t % 3) + 128, T:TPAD], zero[:], pad_stored)
            def stacks(u, tok):
                for s in range(8):
                    rows = slice(16 * s, 16 * s + 16)
                    load(q_st[u][rows], parts_dram[Q_PART[s], 0:C, bass.ds(tok, QW)]
                         .rearrange("(h d) n -> d h n", d=D), stack_in[u])
                    load(k_st[u][rows], parts_dram[K_PART[s], C:2 * C, bass.ds(tok, N)]
                         .rearrange("(h d) n -> d h n", d=D), stack_in[u])

            for n in range(NBLK):
                sp.wait_ge(part_c, 3 * n + 3)
                for k in range(3):
                    load(parts_dram[k, :, n * BLK:(n + 1) * BLK].rearrange("(t p) n -> p t n", p=128),
                         part[n % 2][:, 3 * k:3 * k + 3, :], parts_stored[n % 2])
                if n == 1:
                    sp.wait_ge(parts_stored[0], 48)
                if n in (1, 2):
                    load(hn_b[n - 1][:], hn[:, :, (n - 1) * N:(n - 1) * N + QW], hnb_in[n - 1])
                    stacks(n - 1, (n - 1) * N)

            for u in range(2):
                sp.wait_ge(parts_stored[u], 48 * NBLK // 2)
            sp.wait_ge(pad_stored, 16 * 9)
            sp.wait_ge(hn_done, NBLK)
            sp.wait_ge(xn_tp, NBLK)
            for dst, name in ((wd_raw, "wd_0"), (wd_1_raw[0:F1], "wd_1"), (wd_1_raw[F1:], "wd_1"),
                              (w1_raw, "w1_0"), (w1_1_raw[0:F1], "w1_1"), (w1_1_raw[F1:], "w1_1"),
                              (w_up[:], "w_up")):
                load(dst, a[name], expert_w_in)

            def loads(it, first, last):
                for u in range(2):
                    if first:
                        continue
                    tok = it * (2 * N) + u * N
                    wait(sp, v_mm, 2 * it + u - 1)
                    wait(sp, s_mm, PER * it + PAIRS * (u - 1))
                    load(hn_b[u][:], hn[:, :, bass.ds(tok, QW)], hnb_in[u])
                    stacks(u, tok)

            looped(sp, loads)

            out_v = out.rearrange("(t p) c -> p t c", p=TT)
            sp.wait_ge(y_done, 1)
            sp.dma_start(out_v[:, 0:SUB, :], y_out[:]).then_inc(y_stored, 16)
            with sp.Fori(1, NBLK, 1) as i:
                sp.wait_ge(y_done, i + 1)
                sp.dma_start(out_v[:, bass.ds(i * SUB, SUB), :], y_out[:]).then_inc(y_stored, 16)
            sp.wait_ge(y_stored, 16 * NBLK)

        @block.tensor
        def _(pe):
            mm, tp = nc.tensor.matmul, nc.tensor.transpose

            for i in range(IMG_BLKS):
                pe.wait_ge(patch_in[i], 16 if i else 48)
                for m in range(2):
                    for k in range(KP):
                        last = mm(bank[2 * i + m][0:CP, 0:IMG_N], w_tok[:, k, CP * m:CP * m + CP],
                                  x_patch[:, k, IMG_N * i:IMG_N * (i + 1)], start=(k == 0), stop=(k == KP - 1))
                    last.then_inc(embed_mm, 1)
            for i in range(TXT_BLKS):
                pe.wait_ge(onehot_done, i + 1)
                for m in range(2):
                    q = 2 * i + m
                    if q >= 3:
                        pe.wait_ge(embed_txt, q - 2)
                    mm(bank[TXT_BANK[q % 3]][0:CP, 0:512], table[:, CP * m:CP * m + CP],
                       onehot[:, 512 * i:512 * i + 512], start=True, stop=True).then_inc(embed_mm, 1)

            def norm_in(base, n):
                u = n % 2
                if base:
                    pe.wait_ge(h_added, batches_before((n + 1) * BLK))
                else:
                    pe.wait_ge(embed_img, 2 * IMG_BLKS)
                    pe.wait_ge(embed_txt, 2 * TXT_BLKS)
                if n >= 2:
                    pe.wait_ge(hn_done, base + n - 1)
                    if base:
                        pe.wait_ge(x_lo_done, n - 1)
                for s in range(SUB):
                    t = SUB * n + s
                    for c in range(2):
                        last = tp(bank[2 * u + s // 2][0:TT, C * (s % 2) + CP * c:][:, 0:CP],
                                  hT[:, c, TT * t:TT * t + TT], ident[0:CP, 0:CP])
                last.then_inc(h_tp, 1)

            def norm_out(base, n):
                u = n % 2
                pe.wait_ge(xn_done, base + n + 1)
                if base:
                    pe.wait_ge(h2_out, n + 1)
                chunks = ([(0, 0, F0), (1, F1, C), (1, F0, C)] if base else [(0, 0, CP), (1, CP, C)])
                for s in range(SUB):
                    for c, lo, hi in chunks:
                        last = tp(bank[2 * u + c][0:hi - lo, TT * s:TT * s + TT], xn[:, SUB * n + s, lo:hi],
                                  ident[0:TT, 0:TT])
                last.then_inc(xn_tp, 1)

            pe.wait_ge(early_in, 16)
            norm_in(0, 0)
            norm_in(0, 1)
            for n in range(NBLK + 1):
                if n < NBLK:
                    norm_out(0, n)
                if n >= 1:
                    pe.wait_ge(hn_done, n)
                    for t in range(3):
                        q = 3 * (n - 1) + t
                        if q >= 3:
                            pe.wait_ge(rest_a, q - 2)
                        for c in range(2):
                            last = mm(bank[4 + t][:, 0:BLK], w_qk[:, c, 128 * t:128 * t + 128],
                                      hn[:, c, (n - 1) * BLK:n * BLK], start=(c == 0), stop=(c == 1))
                        last.then_inc(qk_mm, 1)
                if n + 2 < NBLK:
                    norm_in(0, n + 2)
            pe.wait_ge(late_in, 16 * LATE_DMAS)
            pe.wait_ge(rest_a, 3 * NBLK)

            def attention(it, first, last_it):
                def live(k, unit=1):
                    return (not first or k >= 0) and (not last_it or k < PER // unit)

                def scores(k):
                    h, u = 2 * (k % PAIRS), k // PAIRS % 2
                    if k % PAIRS == 0:
                        pe.wait_ge(stack_in[u], it * 256 + 256 * (k // PAIRS // 2 + 1))
                    wait(pe, exp1_b, PER * it + k)
                    for e in range(2):
                        last = mm(bank[2][64 * e:64 * e + 64, 0:N], q_st[u][:, h + e, 128:QW],
                                  k_st[u][:, h + e, :], start=True, stop=True)
                    last.then_inc(s_mm_b, 1)
                    wait(pe, exp1_a, PER * it + k - 1)
                    o = bank[k % 2]
                    mm(o[:, 0:N], q_st[u][:, h, 0:128], k_st[u][:, h, :], start=True, stop=True)
                    mm(o[:, N:N + REST], q_st[u][:, h + 1, 0:128], k_st[u][:, h + 1, 128:N], start=True, stop=True)
                    mm(o[:, N + REST:2 * N], q_st[u][:, h + 1, 0:128], k_st[u][:, h + 1, 0:128],
                       start=True, stop=True).then_inc(s_mm, 1)

                def transposes(k):
                    pe.wait_ge(att_done, PER * it + k + 1)
                    wait(pe, exp2_done, PER * it + k)
                    t = att[k % 2]
                    rest_ = t[:, AT2:AT2 + 192]
                    tp(bank[3][:, 0:128], t[:, 0:128], ident[:])
                    tp(bank[3][:, 128:128 + PW], rest_[0:PW, 0:128], ident[0:PW, 0:PW])
                    tp(bank[3][:, 128 + PW:T0W], t[:, AT1 + REST:AT1 + N], ident[:])
                    tp(bank[4][:, 64:N], rest_[0:PW, 64:192], ident[0:PW, 0:PW])
                    tp(bank[4][0:64, 128:128 + PW], rest_[0:PW, 128:192], ident[0:PW, 0:PW])
                    tp(bank[4][:, 0:128], t[:, 128:256], ident[:]).then_inc(tr_mm, 1)

                def values(g):
                    b, u = g // GROUPS, g // GROUPS % 2
                    pe.wait_ge(exp2_done, PER * it + 2 * g + 2)
                    wait(pe, o_out, PER // 2 * it + g)
                    if g % GROUPS == 0:
                        pe.wait_ge(v_out, 2 * it + b + 1)
                    p = [(2 * g + pair) % 4 for pair in range(2)]
                    parts = ([(j, slice(0, N), 0) if j % 2 == 0 else (j, slice(0, 128), 128 + PW) for j in range(4)]
                             + [(j, slice(128, N), 192) for j in (1, 3)])
                    for n, (j, dst, at) in enumerate(parts):
                        mm(bank[5][32 * j:32 * j + 32, dst], v_lo[u][:, 4 * (g % GROUPS) + j, :],
                           p_lo[p[j // 2]][:, at:at + dst.stop - dst.start], start=(n < 4), stop=False)
                    for n, (j, dst, at) in enumerate(parts):
                        last = mm(bank[5][32 * j:32 * j + 32, dst], v_hi[u][:, 4 * (g % GROUPS) + j, :],
                                  p_hi[p[j // 2]][:, dst], start=False, stop=(j % 2 == 0 or n >= 4))
                    last.then_inc(pv_mm, 1)

                def sums(g):
                    pe.wait_ge(o_out, PER // 2 * it + g + 1)
                    wait(pe, onorm_done, PER // 2 * it + g)
                    tp(bank[6][:, 0:128], o_raw[g % 2][:, 0:128], ident[:])
                    tp(bank[6][0:REST, 128:256], o_raw[g % 2][:, 128:N], ident[:]).then_inc(sum2_tp, 1)

                def sums_back(g):
                    pe.wait_ge(rep_done, PER // 2 * it + g + 1)
                    rep = rsum2_rep[:].rearrange("p c j d -> p c (j d)")
                    tp(bank[6][:, 256:384], rep[:, 0, :], ident[:])
                    tp(bank[6][:, 384:384 + REST], rep[0:REST, 1, :], ident[0:REST, 0:REST]).then_inc(rsum2_tp, 1)

                def v_proj(b):
                    u = b % 2
                    pe.wait_ge(hnb_in[u], it * 16 + 16 * (b // 2) + 16)
                    wait(pe, h_added, 2 * it + b - 1)
                    halves = w_v[:, :, :].rearrange("p c (i e d) -> p c e i d", e=2, d=D)
                    for c in range(2):
                        mm(bank[7][:, 0:C], hn_b[u][:, c, 0:128], w_v[:, c, :], start=(c == 0), stop=(c == 1))
                    for e in range(2):
                        for c in range(2):
                            last = mm(bank[7][64 * e:64 * e + 64, C:C + CP], hn_b[u][:, c, 128:QW],
                                      halves[:, c, e], start=(c == 0), stop=(c == 1))
                    last.then_inc(v_mm, 1)

                def out_proj(b):
                    pe.wait_ge(onorm_done, PER // 2 * it + GROUPS * b + GROUPS)
                    pe.wait_ge(v_out, 2 * it + (min(b + 2, 2) if last_it else b + 2))
                    for m in range(2):
                        for g in range(GROUPS):
                            last = mm(bank[7][0:CP, N * m:N * m + N], w_o[:, g, CP * m:CP * m + CP],
                                      o_norm[b % 2][:, g, :], start=(g == 0), stop=(g == GROUPS - 1))
                    last.then_inc(proj_mm, 1)

                for s in pair_steps(first, last_it):
                    if live(s + 2):
                        scores(s + 2)
                    if live(s):
                        transposes(s)
                    if s % 2 == 0 and live((s - 2) // 2, 2):
                        values((s - 2) // 2)
                    if s % 2 == 1 and live((s - 3) // 2, 2):
                        sums((s - 3) // 2)
                    if s % 2 == 0 and live((s - 4) // 2, 2):
                        sums_back((s - 4) // 2)
                    if s % PAIRS == 5 and live((s + 1) // PAIRS, PAIRS):
                        v_proj((s + 1) // PAIRS)
                    if s % PAIRS == 3 and live((s - 9) // PAIRS, PAIRS):
                        out_proj((s - 9) // PAIRS)

            looped(pe, attention)

            def split_products(dst, cols, w_hi, w_lo, w_1, tokens):
                pairs = ((w_hi, x_hi), (w_lo, x_hi), (w_hi, x_lo), (w_1, x1_hi), (w_1, x1_lo))
                for n, (w, x) in enumerate(pairs):
                    last = mm(dst, w[:, cols], x[:, tokens], start=(n == 0), stop=(n == len(pairs) - 1))
                return last

            norm_in(NBLK, 0)
            norm_in(NBLK, 1)
            pe.wait_ge(w_lo_done, 2 * NWCHUNK + 2)
            for n in range(NBLK + 2):
                if n < NBLK:
                    norm_out(NBLK, n)
                if n >= 2:
                    pe.wait_ge(g1_done, n - 1)
                    wait(pe, logit_done, n - 2)
                    for s in range(SUB):
                        last = mm(bank[6][0:TT, E * s:E * s + E], g1[(n - 1) % 2][:, TT * s:TT * s + TT], w2,
                                  start=True, stop=True)
                    last.then_inc(logit_mm, 1)
                if 1 <= n <= NBLK:
                    pe.wait_ge(hn_done, NBLK + n)
                    pe.wait_ge(x_lo_done, n)
                    split_products(bank[4 + (n - 1) % 2][0:CP, 0:BLK], slice(0, CP), w1_hi, w1_lo, w1_1,
                                   slice((n - 1) * BLK, n * BLK)).then_inc(g1_mm, 1)
                if n + 2 < NBLK:
                    norm_in(NBLK, n + 2)

            pe.wait_ge(expert_w_in, 16 * 7)
            pe.wait_ge(logit_done, NBLK)

            def experts(i, first):
                def down(e):
                    for half in range(2):
                        q = 2 * e + half
                        if not (first and q < 4):
                            pe.wait_ge(z_done, 2 * E * i + q - 3)
                        at = ED * e + 128 * half
                        split_products(bank[q % 4][:, 0:BLK], slice(at, at + 128), wd_hi, wd_lo, wd_1,
                                       bass.ds(i * BLK, BLK)).then_inc(down_mm, 1)

                def up(e):
                    pe.wait_ge(z_done, 2 * E * i + 2 * e + 2)
                    if not (first and e < 2):
                        pe.wait_ge(acc_done, E * i + e - 1)
                    for s in range(SUB):
                        for half in range(2):
                            last = mm(bank[4 + 2 * (e % 2) + s // 2][0:TT, C * (s % 2):C * (s % 2) + C],
                                      z[e % 2][:, half, TT * s:TT * s + TT], w_up[:, 2 * e + half, :],
                                      start=(half == 0), stop=(half == 1))
                    last.then_inc(up_mm, 1)

                down(0)
                for e in range(E):
                    if e + 1 < E:
                        down(e + 1)
                    up(e)

            experts(0, True)
            with pe.Fori(1, NBLK, 1) as i:
                experts(i, False)

        @block.scalar
        def _(act):
            fn = nc.scalar.activation
            act.wait_ge(patch_in[0], 48)
            for i in range(IMG_BLKS):
                for m in range(2):
                    act.wait_ge(embed_mm, 2 * i + m + 1)
                    dst = hT[:, m, i * 8 * N:(i + 1) * 8 * N].rearrange("p (b n) -> p b n", n=N)[:, :, 0:NI]
                    fn(dst, bank[2 * i + m][0:CP, 0:IMG_N].rearrange("p (b n) -> p b n", n=NI), ACT.Identity,
                       bias=b_tok[:, m:m + 1]).then_inc(embed_img, 1)

            def residual(n):
                act.wait_ge(n_stat, NBLK + n + 1)
                for s in range(0, SUB, 2):
                    ins = fn(h2b[:, SUB * n + s:SUB * n + s + 2, :], bank[2 * (n % 2) + s // 2][0:TT, 0:2 * C], ACT.Copy)
                ins.then_inc(h2_out, 1)

            act.wait_ge(early_in, 16)
            for n in range(NBLK + 1):
                if n < NBLK:
                    act.wait_ge(xn_tp, n + 1)
                    for c in range(2):
                        ins = fn(hn[:, c, n * BLK:(n + 1) * BLK], bank[2 * (n % 2) + c][0:CP, 0:BLK], ACT.Copy)
                    ins.then_inc(hn_done, 1)
                if n >= 1:
                    u = (n - 1) % 2
                    if n >= 3:
                        act.wait_ge(parts_stored[u], 48 * ((n - 1) // 2))
                    for t in range(3):
                        q = 3 * (n - 1) + t
                        act.wait_ge(qk_mm, q + 1)
                        fn(part[u][:, t, :], bank[4 + t][:, 0:BLK], ACT.Copy,
                           scale=qk_scale[:, t:t + 1]).then_inc(part_a, 1)
                        act.wait_ge(rest_a, q + 1)
                        fn(part[u][:, 3 + t, :], rest[u][:, t, :], ACT.Copy).then_inc(part_b, 1)

            def attention(it, first, last_it):
                def live(k, unit=1):
                    return (not first or k >= 0) and (not last_it or k < PER // unit)

                def exp1(k, units):
                    src = [bank[k % 2][:, 0:N], bank[k % 2][:, N:2 * N], bank[2][:, 0:N]]
                    for w in units:
                        ins = fn(e1[k % 2][:, w, :], src[w], ACT.Exp, bias=neg_max[k % 2][:, w:w + 1],
                                 accum_out=sum1[k % 2][:, w:w + 1])
                    return ins

                def exp2(k):
                    act.wait_ge(tr_mm, PER * it + k + 1)
                    wait(act, pv_mm, PER // 2 * it + k // 2 - 1)
                    fn(p_lo[k % 4][:], bank[3][:, 0:T0W], ACT.Exp)
                    fn(p_hi[k % 4][:], bank[4][:, 0:N], ACT.Exp).then_inc(exp2_done, 1)

                def out_raw(g):
                    act.wait_ge(pv_mm, PER // 2 * it + g + 1)
                    wait(act, onorm_done, PER // 2 * it + g - 1)
                    fn(o_raw[g % 2][:], bank[5][:, 0:N], ACT.Copy).then_inc(o_out, 1)

                def v_copy(b):
                    act.wait_ge(v_mm, 2 * it + b + 1)
                    fn(v_lo[b % 2][:, :, 0:D], bank[7][:, 0:C].rearrange("p (h d) -> p h d", d=D), ACT.Copy)
                    for e in range(2):
                        rows = slice(64 * e, 64 * e + REST)
                        ins = fn(v_hi[b % 2][rows, e::2, 0:D],
                                 bank[7][rows, C:C + CP].rearrange("p (h d) -> p h d", d=D), ACT.Copy)
                    ins.then_inc(v_out, 1)

                for s in pair_steps(first, last_it):
                    if s % 2 == 1 and live((s - 3) // 2, 2):
                        out_raw((s - 3) // 2)
                    if s % PAIRS == 0 and live(s // PAIRS, PAIRS):
                        v_copy(s // PAIRS)
                    if live(s + 2):
                        act.wait_ge(max_b, PER * it + s + 3)
                        exp1(s + 2, (2,)).then_inc(exp1_b, 1)
                    if live(s):
                        exp2(s)
                    if live(s + 2):
                        act.wait_ge(max_done, PER * it + s + 3)
                        exp1(s + 2, (0, 1)).then_inc(exp1_a, 1)

            looped(act, attention)

            for u in range(2):
                act.wait_ge(hnb_in[u], 16 * B // 2)
            residual(0)
            for n in range(NBLK + 1):
                if n < NBLK:
                    act.wait_ge(xn_tp, NBLK + n + 1)
                    for c, dst in enumerate((x_hi, x1_hi)):
                        ins = fn(dst[:, n * BLK:(n + 1) * BLK], bank[2 * (n % 2) + c][:, 0:BLK], ACT.Copy)
                    ins.then_inc(hn_done, 1)
                if n + 1 < NBLK:
                    residual(n + 1)
                if n >= 1:
                    act.wait_ge(g1_mm, n)
                    fn(g1[n % 2][:], bank[4 + (n - 1) % 2][0:CP, 0:BLK], ACT.Gelu, bias=b1).then_inc(g1_done, 1)
            act.wait_ge(route_dve, 1)
            fn(expl[:], shifted[:], ACT.Exp).then_inc(route_exp, 1)

            act.wait_ge(rank_done, NBLK)

            def experts(i, first):
                for e in range(E):
                    for half in range(2):
                        act.wait_ge(down_mm, 2 * E * i + 2 * e + half + 1)
                        if half == 0 and not (first and e < 2):
                            act.wait_ge(up_mm, E * i + e - 1)
                        fn(z[e % 2][:, half, :], bank[(2 * e + half) % 4][:, 0:BLK], ACT.Gelu,
                           bias=down_b[:, 2 * e + half:2 * e + half + 1]).then_inc(z_done, 1)

            experts(0, True)
            with act.Fori(1, NBLK, 1) as i:
                experts(i, False)

        @block.vector
        def _(dve):
            v = nc.vector
            v.memset(hn[:, :, T:TPAD], 0.0)
            v.memset(one[:], 1.0)
            for u in range(2):
                v.memset(v_lo[u][:], 1.0)
                v.memset(v_hi[u][:], 0.0)
                v.memset(att[u][:], 0.0)
            v.memset(bank[6][:], 1.0).then_inc(zeroed, 1)
            dve.wait_ge(zeroed, 1)
            for u in range(2):
                for e in range(2):
                    v.memset(v_hi[u][64 * e:64 * e + REST, e::2, D:2 * D], 1.0)
            v.memset(zero[:], 0.0).then_inc(preset, 1)

            dve.wait_ge(text_in, 16 * TEXT_DMAS)
            for i in range(TXT_BLKS):
                cols = slice(512 * i, 512 * i + 512)
                v.tensor_scalar(onehot[:, cols], tok_i[:, cols], float(VOC - 1), iota[:, 0:1], ALU.min, ALU.is_equal)\
                    .then_inc(onehot_done, 1)
            for i in range(TXT_BLKS):
                for m in range(2):
                    q = 2 * i + m
                    dve.wait_ge(embed_mm, 2 * IMG_BLKS + q + 1)
                    dst = hT[:, m, i * TXT_B * N:(i + 1) * TXT_B * N].rearrange("p (b n) -> p b n", n=N)[:, :, NI:N]
                    v.scalar_tensor_tensor(
                        out=dst, in0=bank[TXT_BANK[q % 3]][0:CP, :].rearrange("p (b n) -> p b n", n=NT),
                        scalar=float(C) ** 0.5, in1=pe_sb[:, m, :].unsqueeze(1).to_broadcast([CP, TXT_B, NT]),
                        op0=ALU.mult, op1=ALU.add).then_inc(embed_txt, 1)

            def statistics(base, n):
                k, t0 = base + n + 1, SUB * n
                dve.wait_ge(h_tp, k)
                for s in range(SUB):
                    ins = v.bn_stats(n_stats[:, t0 + s, :],
                                     bank[2 * (n % 2) + s // 2][0:TT, C * (s % 2):C * (s % 2) + C])
                ins.then_inc(n_stat, 1)
                dve.wait_ge(n_stat, k)
                for s in range(SUB):
                    ins = v.bn_aggr(n_mv[:, t0 + s, :], n_stats[:, t0 + s, :])
                ins.then_inc(n_mv_done, 1)

            def normalised(base, n):
                dve.wait_ge(n_rstd_done, base + n + 1)
                if base:
                    dve.wait_ge(h2_out, n + 1)
                for s in range(SUB):
                    t = SUB * n + s
                    src = bank[2 * (n % 2) + s // 2][0:TT, C * (s % 2):C * (s % 2) + C]
                    ins = v.tensor_scalar(xn[:, t, :], src, n_mv[:, t, 0:1], n_rstd[:, t:t + 1],
                                          ALU.subtract, ALU.mult)
                ins.then_inc(xn_done, 1)

            dve.wait_ge(early_in, 16)
            statistics(0, 0)
            normalised(0, 0)
            for n in range(NBLK + 1):
                if n + 1 < NBLK:
                    statistics(0, n + 1)
                    normalised(0, n + 1)
                if n >= 1:
                    u = (n - 1) % 2
                    for t in range(3):
                        dve.wait_ge(part_a, 3 * (n - 1) + t + 1)
                        if n >= 3 and t == 0:
                            dve.wait_ge(part_c, 3 * (n - 2))
                        v.scalar_tensor_tensor(
                            out=rest[u][:, t, :], in0=bank[4 + t][:, 0:BLK], scalar=qk_scale[:, t:t + 1],
                            in1=part[u][:, t, :], op0=ALU.mult, op1=ALU.subtract).then_inc(rest_a, 1)
            dve.wait_ge(late_in, 16 * LATE_DMAS)

            def attention(it, first, last_it):
                def live(k, unit=1):
                    return (not first or k >= 0) and (not last_it or k < PER // unit)

                def maxima(k):
                    dve.wait_ge(s_mm_b, PER * it + k + 1)
                    v.tensor_reduce(neg_max[k % 2][:, 2:3], bank[2][:, 0:N], AX_X, ALU.max, negate=True)\
                        .then_inc(max_b, 1)
                    dve.wait_ge(s_mm, PER * it + k + 1)
                    v.tensor_reduce(neg_max[k % 2][:, 0:2], bank[k % 2][:, 0:2 * N].rearrange("p (e n) -> p e n", e=2),
                                    AX_X, ALU.max, negate=True).then_inc(max_done, 1)

                def normalise(k):
                    dve.wait_ge(exp1_a, PER * it + k + 1)
                    v.reciprocal(rsum1[k % 2][:], sum1[k % 2][:]).then_inc(rsum_done, 1)
                    wait(dve, tr_mm, PER * it + k - 1)
                    dve.wait_ge(rsum_done, PER * it + k + 1)
                    for w, (at, mask) in enumerate(((0, mask_a), (AT1, mask_r), (AT2, mask_b))):
                        ins = v.scalar_tensor_tensor(
                            out=att[k % 2][:, at:at + N], in0=e1[k % 2][:, w, :],
                            scalar=rsum1[k % 2][:, w:w + 1], in1=mask[:], op0=ALU.mult, op1=ALU.mult)
                    ins.then_inc(att_done, 1)

                def reciprocals(g):
                    dve.wait_ge(sum2_tp, PER // 2 * it + g + 1)
                    wait(dve, rep_done, PER // 2 * it + g)
                    sums = bank[6][:, 0:256].rearrange("p (c j d) -> p c j d", c=2, j=4)[:, :, :, D]
                    v.reciprocal(rsum2[:], sums).then_inc(rsum2_done, 1)

                def scale_out(g):
                    dve.wait_ge(rsum2_tp, PER // 2 * it + g + 1)
                    v.tensor_tensor(o_norm[g // GROUPS % 2][:, g % GROUPS, :], o_raw[g % 2][:],
                                    bank[6][:, 256:256 + N], ALU.mult).then_inc(onorm_done, 1)

                def add_out(b):
                    dve.wait_ge(proj_mm, 2 * it + b + 1)
                    for m in range(2):
                        h = hT[:, m, bass.ds(it * (2 * N) + b * N, N)]
                        ins = v.scalar_tensor_tensor(out=h, in0=bank[7][0:CP, N * m:N * m + N],
                                                     scalar=b_o[:, m:m + 1], in1=h, op0=ALU.add, op1=ALU.add)
                    ins.then_inc(h_added, 1)

                for s in pair_steps(first, last_it):
                    if s % 2 == 1 and live((s - 5) // 2, 2):
                        scale_out((s - 5) // 2)
                    if s % 2 == 0 and live((s - 4) // 2, 2):
                        reciprocals((s - 4) // 2)
                    if s % PAIRS == 4 and live((s - 10) // PAIRS, PAIRS):
                        add_out((s - 10) // PAIRS)
                    if live(s + 2):
                        maxima(s + 2)
                    if live(s + 1):
                        normalise(s + 1)

            looped(dve, attention)

            def logits(n):
                dve.wait_ge(logit_mm, n + 1)
                v.tensor_tensor(logit[:, SUB * n:SUB * n + SUB, :],
                                bank[6][0:TT, 0:SUB * E].rearrange("p (s e) -> p s e", e=E),
                                b2[:].unsqueeze(1).to_broadcast([TT, SUB, E]), ALU.add).then_inc(logit_done, 1)

            def compare(n):
                t = slice(SUB * n, SUB * n + SUB)
                shape = [TT, SUB, E, E]
                dve.wait_ge(logit_done, n + 1)
                v.tensor_tensor(cmp_ge[:, t], logit[:, t].unsqueeze(2).to_broadcast(shape),
                                logit[:, t].unsqueeze(3).to_broadcast(shape), ALU.is_ge).then_inc(compared, 1)

            def ranks(n):
                t = slice(SUB * n, SUB * n + SUB)
                dve.wait_ge(ahead_done, n + 1)
                v.tensor_reduce(rank[:, t], cmp_ge[:, t], AX_X, ALU.add)
                v.tensor_reduce(behind[:, t], cmp_ge[:, t].rearrange("p t e j -> p t j e"), AX_X, ALU.add)\
                    .then_inc(rank_done, 1)

            statistics(NBLK, 0)
            normalised(NBLK, 0)
            for n in range(NBLK + 2):
                if n + 1 < NBLK:
                    statistics(NBLK, n + 1)
                if n < NBLK:
                    dve.wait_ge(hn_done, NBLK + n + 1)
                    cols = slice(n * BLK, (n + 1) * BLK)
                    for c, (lo, hi) in enumerate(((x_lo, x_hi), (x1_lo, x1_hi))):
                        ins = v.tensor_tensor(lo[:, cols], bank[2 * (n % 2) + c][:, 0:BLK], hi[:, cols].bitcast(F32),
                                              ALU.subtract)
                    ins.then_inc(x_lo_done, 1)
                if n + 1 < NBLK:
                    normalised(NBLK, n + 1)
                if n >= 2:
                    logits(n - 2)
                    compare(n - 2)
                if n >= 3:
                    ranks(n - 3)
            ranks(NBLK - 1)
            dve.wait_ge(logit_done, NBLK)
            v.tensor_reduce(top[:], logit[:], AX_X, ALU.max).then_inc(fin_dve, 1)
            dve.wait_ge(fin_dve, 1)
            v.tensor_tensor(shifted[:], logit[:], top[:].unsqueeze(2).to_broadcast([TT, NTILE, E]),
                            ALU.subtract).then_inc(route_dve, 1)
            dve.wait_ge(rank_done, NBLK)
            v.tensor_tensor(rank[:], rank[:], behind[:], ALU.subtract).then_inc(fin_dve, 1)
            dve.wait_ge(fin_dve, 2)
            v.tensor_tensor(rank[:], rank[:], later.unsqueeze(1).to_broadcast([TT, NTILE, E]), ALU.add)\
                .then_inc(fin_dve, 1)
            dve.wait_ge(fin_dve, 3)
            dve.wait_ge(route_exp, 1)
            v.scalar_tensor_tensor(out=kept[:].rearrange("p t e -> p (t e)"), in0=rank[:].rearrange("p t e -> p (t e)"),
                                   scalar=1.5, in1=expl[:].rearrange("p t e -> p (t e)"),
                                   op0=ALU.is_lt, op1=ALU.mult).then_inc(fin_dve, 1)
            v.tensor_reduce(sum_e[:], expl[:], AX_X, ALU.add).then_inc(fin_dve, 1)
            dve.wait_ge(fin_dve, 4)
            v.tensor_reduce(sum_k[:], kept[:], AX_X, ALU.add).then_inc(fin_dve, 1)
            dve.wait_ge(fin_dve, 6)
            v.scalar_tensor_tensor(out=sum_k[:], in0=sum_e[:], scalar=GATE_EPS, in1=sum_k[:],
                                   op0=ALU.mult, op1=ALU.add).then_inc(fin_dve, 1)
            dve.wait_ge(fin_dve, 7)
            v.reciprocal(sum_e[:], sum_k[:]).then_inc(fin_dve, 1)
            dve.wait_ge(fin_dve, 8)
            v.tensor_tensor(gate[:], kept[:], sum_e[:].unsqueeze(2).to_broadcast([TT, NTILE, E]),
                            ALU.mult).then_inc(fin_dve, 1)
            dve.wait_ge(fin_dve, 9)

            def experts(i, first):
                v.tensor_copy(gate_b[:], gate[:, bass.ds(i * SUB, SUB), :]).then_inc(gate_cp, 1)
                wait(dve, y_done, i)
                dve.wait_ge(gate_cp, i + 1)
                for e in range(E):
                    dve.wait_ge(up_mm, E * i + e + 1)
                    wait(dve, acc_done, E * i + e)
                    for s in range(SUB):
                        before = acc[:, s, :] if e else xn[:, bass.ds(i * SUB + s, 1), :].squeeze(1)
                        ins = v.scalar_tensor_tensor(
                            out=acc[:, s, :], in0=bank[4 + 2 * (e % 2) + s // 2][0:TT, C * (s % 2):C * (s % 2) + C],
                            scalar=gate_b[:, s, e:e + 1], in1=before, op0=ALU.mult, op1=ALU.add)
                    ins.then_inc(acc_done, 1)
                dve.wait_ge(acc_done, E * i + E)
                for s in range(SUB):
                    ins = v.bn_stats(stats[:, s, :], acc[:, s, :])
                ins.then_inc(fin_dve, 1)
                dve.wait_ge(fin_dve, 10 + 3 * i)
                dve.sem_inc(stats_seen, 1)
                for s in range(SUB):
                    ins = v.bn_aggr(mv[:, s, :], stats[:, s, :])
                ins.then_inc(mv_done, 1)
                dve.wait_ge(rstdy_done, i + 1)
                dve.wait_ge(mv_done, i + 1)
                for s in range(SUB):
                    ins = v.tensor_scalar(acc[:, s, :], acc[:, s, :], mv[:, s, 0:1], rstd_y[:, s:s + 1],
                                          ALU.subtract, ALU.mult)
                ins.then_inc(fin_dve, 1)
                dve.wait_ge(fin_dve, 11 + 3 * i)
                v.tensor_tensor(acc, acc, gamma[:].unsqueeze(1).to_broadcast([TT, SUB, C]), ALU.mult)\
                    .then_inc(fin_dve, 1)
                dve.wait_ge(fin_dve, 12 + 3 * i)
                dve.wait_ge(h2b_done, 1)
                wait(dve, y_stored, 16 * i)
                v.tensor_tensor(y_out[:], acc, h2b[:, bass.ds(i * SUB, SUB), :], ALU.add).then_inc(y_done, 1)

            experts(0, True)
            with dve.Fori(1, NBLK, 1) as i:
                experts(i, False)

        @block.gpsimd
        def _(pool):
            g = nc.gpsimd

            def deviation(base, n):
                k, t = base + n + 1, slice(SUB * n, SUB * n + SUB)
                pool.wait_ge(n_mv_done, k)
                g.tensor_tensor(n_var[:, t], n_mv[:, t, 1], eps.to_broadcast([TT, SUB]), ALU.add)\
                    .then_inc(n_var_done, 1)
                pool.wait_ge(n_var_done, k)
                g.tensor_tensor(n_rstd[:, t], n_var[:, t], neg_half[0:TT, :].to_broadcast([TT, SUB]), ALU.pow)\
                    .then_inc(n_rstd_done, 1)

            pool.wait_ge(preset, 1)
            pool.wait_ge(early_in, 16)
            deviation(0, 0)
            for n in range(NBLK + 1):
                if n + 1 < NBLK:
                    deviation(0, n + 1)
                if n >= 1:
                    u = (n - 1) % 2
                    for t in range(3):
                        pool.wait_ge(part_b, 3 * (n - 1) + t + 1)
                        g.tensor_tensor(part[u][:, 6 + t, :], rest[u][:, t, :], part[u][:, 3 + t, :],
                                        ALU.subtract).then_inc(part_c, 1)

            def split_weights(n, hi, lo, raw, hi_lo, raw_1):
                ones = one[:].to_broadcast([128, raw.shape[-1]])
                g.tensor_tensor(hi, raw, ones, ALU.mult).then_inc(w_hi_done, 1)
                g.tensor_tensor(hi_lo, raw_1, ones, ALU.mult).then_inc(w_hi_done, 1)
                pool.wait_ge(w_hi_done, 2 * n + 1)
                g.tensor_tensor(lo, raw, hi.bitcast(F32), ALU.subtract).then_inc(w_lo_done, 1)
                pool.wait_ge(w_lo_done, 2 * n + 1)
                g.tensor_tensor(hi_lo[F1:], raw_1[F1:], hi_lo[F1:].bitcast(F32), ALU.subtract).then_inc(w_lo_done, 1)
                pool.wait_ge(w_lo_done, 2 * n + 2)

            def split_chunk(n):
                if n < NWCHUNK:
                    c = slice(WCHUNK * n, WCHUNK * (n + 1))
                    split_weights(n, wd_hi[:, c], wd_lo[:, c], wd_raw[:, c], wd_1[:, c], wd_1_raw[:, c])
                elif n == NWCHUNK:
                    split_weights(n, w1_hi[:], w1_lo[:], w1_raw, w1_1[:], w1_1_raw)

            def attention(it, first, last_it):
                for j in range(PER // 2):
                    pool.wait_ge(rsum2_done, PER // 2 * it + j + 1)
                    wait(pool, rsum2_tp, PER // 2 * it + j)
                    g.tensor_tensor(rsum2_rep[:].rearrange("p c j d -> p (c j) d"),
                                    rsum2[:].rearrange("p c j -> p (c j)").unsqueeze(2).to_broadcast([128, 8, 2 * D]),
                                    one[:].unsqueeze(2).to_broadcast([128, 8, 2 * D]), ALU.mult)\
                        .then_inc(rep_done, 1)
                    if first and j >= 2:
                        if j == 2:
                            pool.wait_ge(expert_w_in, 16 * 7)
                        split_chunk(j - 2)
                    if last_it:
                        split_chunk(PER // 2 - 2 + j)

            looped(pool, attention)

            def ahead(n):
                t = slice(SUB * n, SUB * n + SUB)
                pool.wait_ge(compared, n + 1)
                ge = cmp_ge[:, t].rearrange("p t e j -> p t (e j)")
                tri = earlier.rearrange("p e j -> p (e j)").unsqueeze(1).to_broadcast([TT, SUB, E * E])
                g.tensor_tensor(ge, ge, tri, ALU.mult).then_inc(ahead_done, 1)

            pool.wait_ge(late_in, 16 * LATE_DMAS)
            deviation(NBLK, 0)
            for n in range(NBLK + 2):
                if n + 1 < NBLK:
                    deviation(NBLK, n + 1)
                if n >= 2:
                    ahead(n - 2)

            pool.wait_ge(h2_out, NBLK)
            g.tensor_tensor(h2b, h2b, beta[:].unsqueeze(1).to_broadcast([TT, NTILE, C]), ALU.add)\
                .then_inc(h2b_done, 1)

            def experts(i, first):
                pool.wait_ge(mv_done, i + 1)
                g.tensor_tensor(vy[:], mv[:, :, 1], eps[:].to_broadcast([TT, SUB]), ALU.add).then_inc(vy_done, 1)
                pool.wait_ge(vy_done, i + 1)
                g.tensor_tensor(rstd_y[:], vy[:], neg_half[0:TT, :].to_broadcast([TT, SUB]), ALU.pow)\
                    .then_inc(rstdy_done, 1)

            experts(0, True)
            with pool.Fori(1, NBLK, 1) as i:
                experts(i, False)


def constants():
    f = np.float32
    q = np.arange(128)
    k = np.arange(N)
    def mask(rows):
        return np.where((rows % NUM)[:, None] == (k % NUM)[None, :], f(0.5), f(1.0)).astype(f)
    pos = np.arange(NT, dtype=f)[:, None]
    inv = np.exp(-(np.arange(0, C, 2, dtype=f) / f(C)) * f(np.log(10000.0))).astype(f)
    ang = (pos * inv).astype(f)
    pe = np.stack([np.sin(ang), np.cos(ang)], axis=-1).reshape(NT, C).astype(f)
    scale = np.where(np.arange(2 * C) < C, f(D) ** f(-0.5), f(1.0)).astype(f)
    e = np.arange(E)
    return {
        "iota": np.arange(VOC, dtype=f)[:, None],
        "pe": pe.T.reshape(2, CP, NT).transpose(1, 0, 2),
        "eps": np.full((TT, 1), LN_EPS, f),
        "neg_half": np.full((128, 1), -0.5, f),
        "qk_scale": scale.reshape(3, 128).T,
        "ident": np.eye(128, dtype=f),
        "mask_a": mask(q),
        "mask_b": mask(128 + q % 64),
        "mask_r": np.roll(mask(q), REST, axis=1),
        "earlier": np.broadcast_to((e[None, :] < e[:, None]).astype(f), (TT, E, E)),
        "later": np.broadcast_to((E - 1 - e).astype(f), (TT, E)),
    }


def kernel(**inputs):
    import concourse.bacc as bacc
    from concourse.bass_utils import run_bass_kernel_spmd

    i = {k: np.asarray(v) for k, v in inputs.items()}

    def chunks(w):
        return w.reshape(2, CP, -1).transpose(1, 0, 2)

    w_o = np.zeros((4, 32, GROUPS, C), np.float32)
    w_o[:, :D] = i["L0_attn_w_out"].T.reshape(GROUPS, 4, D, C).transpose(1, 2, 0, 3)
    w_down = i["L0_ffn_down_w"].transpose(1, 0, 2).reshape(C, E * ED)
    fields = {
        "w_qk": chunks(i["L0_attn_w_qkv"][:2 * C].T), "w_v": chunks(i["L0_attn_w_qkv"][2 * C:].T),
        "w_o": w_o, "b_o": i["L0_attn_b_out"].reshape(2, CP).T, "b1": i["L0_ffn_b1"].reshape(CP, 1),
        "w2": i["L0_ffn_w2"], "down_b": i["L0_ffn_down_b"].reshape(2 * E, 128).T,
        **constants(),
    }

    def packed(names):
        out = np.zeros((128, sum(words(s) for _, s in names)), np.float32)
        at = 0
        for name, shape in names:
            out[:shape[0], at:at + words(shape)] = fields[name].reshape(shape[0], -1)
            at += words(shape)
        return out

    arrays = {
        "x_patch": i["x"].reshape(B, 3, 7, 2, 8, 7, 16).transpose(4, 6, 1, 3, 0, 2, 5).reshape(128, KP, NPATCH),
        "w_tok": i["L0_tok_W"].reshape(C, 2, 8, 16, 3).transpose(2, 3, 4, 1, 0).reshape(128, KP, C),
        "b_tok": i["L0_tok_b"].reshape(2, CP).T,
        "tokens": i["x_txt"].reshape(B * NT),
        "color": i["L0_txt_color_W"], "shape": i["L0_txt_shape_W"],
        "quantity": i["L0_txt_quantity_W"], "special": i["L0_txt_special_W"],
        "w1_0": i["L0_ffn_w1"][:F0], "w1_1": i["L0_ffn_w1"][F0:], "b2": i["L0_ffn_b2"],
        "wd_0": w_down[:F0], "wd_1": w_down[F0:],
        "w_up": i["L0_ffn_up_w"].reshape(2 * E, 128, C).transpose(1, 0, 2),
        "gamma": i["L0_ffn_gamma"], "beta": i["L0_ffn_beta"],
        "iota": fields["iota"], "pe": fields["pe"],
        "early": packed(EARLY), "late": packed(LATE),
    }
    arrays = {k: np.ascontiguousarray(v) for k, v in arrays.items()}
    nc = bacc.Bacc("TRN2", target_bir_lowering=False, num_devices=1)
    aps = {k: nc.dram_tensor(f"in_{k}", v.shape, mybir.dt.from_np(v.dtype), kind="ExternalInput").ap()
           for k, v in arrays.items()}
    out = nc.dram_tensor("out", (T, C), F32, kind="ExternalOutput").ap()
    build(nc, aps, out)
    r = run_bass_kernel_spmd(nc, [{f"in_{k}": v for k, v in arrays.items()}], core_ids=[0])
    return r.results[0]["out"].reshape(B, N, C)
```

```python
from contextlib import ExitStack

import numpy as np

import concourse.bass as bass
from concourse import mybir

F32 = mybir.dt.float32
BF16 = mybir.dt.bfloat16
F32R = mybir.dt.float32r
I32 = mybir.dt.int32
ALU = mybir.AluOpType
ACT = mybir.ActivationFunctionType
AX_X = mybir.AxisListType.X

B = 16
NI, NT = 49, 128
N = NI + NT
T = B * N
C = 192
CP = C // 2
H, D = 12, 16
NUM = N // 4
KP = 6
NPATCH = B * NI
VOC = 70
E, ED = 8, 256
LN_EPS = 1e-5
GATE_EPS = 1e-8

BLK = 472
NBLK = T // BLK
TT = 118
SUB = BLK // TT
TPAD = T + 16

QW = 192
REST = N - 128
PW = 64 + REST
UNITS = 3
PAIRS = H // 2
NPAIR = B * PAIRS
PER = 2 * PAIRS
NIT = NPAIR // PER
GROUPS = PAIRS // 2
T0W = 128 + PW + 128
AT1 = 192
AT2 = AT1 + N
ATW = AT2 + 192
NTILE = NBLK * SUB
F0, F1 = 128, C - 128
WCHUNK = 256
DRAIN = 5

Q_PART = [0, 0, 0, 1, 1, 1, 2, 2]
K_PART = [0, 1, 2, 0, 1, 2, 0, 1]


EARLY = (("ident", (128, 128)), ("w_qk", (CP, 2, 2 * C)), ("qk_scale", (128, 3)),
         ("neg_half", (128, 1)), ("eps", (TT, 1)))
LATE = (("mask_a", (128, N)), ("mask_r", (128, N)), ("mask_b", (128, N)), ("w_v", (CP, 2, C)),
        ("w_o", (128, GROUPS, C)), ("b_o", (CP, 2)), ("b1", (CP, 1)), ("w2", (CP, E)),
        ("earlier", (TT, E, E)), ("later", (TT, E)), ("euler", (TT, 1)), ("down_b", (128, 2 * E)))


def words(shape):
    return int(np.prod(shape[1:]))


def wait(eng, sem, value):
    if not (isinstance(value, int) and value <= 0):
        eng.wait_ge(sem, value)


def pair_steps(first, last):
    return range(-2 if first else 0, PER + (DRAIN if last else 0))


def looped(eng, body):
    body(0, True, False)
    with eng.Fori(1, NIT - 1, 1) as it:
        body(it, False, False)
    body(NIT - 1, False, True)


def block_loop(eng, body):
    body(0, True, False)
    with eng.Fori(1, NBLK - 1, 1) as i:
        body(i, False, False)
    body(NBLK - 1, False, True)


def build(nc, a, out):
    with ExitStack() as ctx:
        def sb(name, shape, dt=F32, phase=ctx):
            return phase.enter_context(nc.sbuf_tensor(name, shape, dt))

        def sem(name):
            return ctx.enter_context(nc.semaphore(name))

        bank = [ctx.enter_context(nc.psum_tensor(f"bank{i}", [128, 512], F32)) for i in range(8)]
        parts_dram = nc.dram_tensor("qk_parts", (3, 2 * C, TPAD), BF16).ap()

        hT = sb("hT", [CP, 2, T])
        b_tok = sb("b_tok", [CP, 2])
        table = sb("table", [VOC, C])
        iota = sb("iota", [VOC, 1])
        pe_sb = sb("pe_sb", [CP, 2, NT])
        one = sb("one", [128, 1])
        early = sb("early", [128, sum(words(s) for _, s in EARLY)])
        late = sb("late", [128, sum(words(s) for _, s in LATE)])
        w1_hi = sb("w1_hi", [128, CP], F32R)
        w1_lo = sb("w1_lo", [128, CP], F32R)
        w1_1 = sb("w1_1", [128, CP], F32R)
        b2 = sb("b2", [TT, E])
        gamma = sb("gamma", [TT, C])
        beta = sb("beta", [TT, C])
        zero = sb("zero", [128, 16], BF16)

        area_c = sb("area_c", [128, 7264])
        with ExitStack() as until_attention:
            area_b, area_h, area_a, area_d = (
                sb(name, [128, size], phase=until_attention) for name, size in
                (("area_b", 9216), ("area_h", 2 * TPAD), ("area_a", 8960), ("area_d", 5440)))
        wd_hi, wd_lo, wd_1 = (sb(name, [128, E * ED], F32R) for name in ("wd_hi", "wd_lo", "wd_1"))
        w_up = sb("w_up", [128, 2 * E, C])
        x_hi, x_lo, x1_hi, x1_lo = (sb(name, [128, T], F32R) for name in ("x_hi", "x_lo", "x1_hi", "x1_lo"))
        area_e = sb("area_e", [128, 2 * TPAD + 8960 + 5440 - 4 * T])

        def carve(area, at, shape, dt=F32):
            n = int(np.prod(shape[1:]))
            size = n if dt is not BF16 else n // 2
            v = area[0:shape[0], at:at + size]
            if dt is not F32:
                v = v.bitcast(dt)
            names = ["x", "y", "z"][:len(shape) - 1]
            if len(names) > 1:
                v = v.rearrange(f"p ({' '.join(names)}) -> p {' '.join(names)}",
                                **dict(zip(names[1:], shape[2:])))
            return v, at + size

        packed = {}
        for area, fields in ((early, EARLY), (late, LATE)):
            o = 0
            for name, shape in fields:
                packed[name], o = carve(area, o, list(shape))
        (ident, w_qk, qk_scale, neg_half, eps, mask_a, mask_r, mask_b, w_v, w_o, b_o, b1, w2, earlier, later, euler,
         down_b) = (packed[name] for name, _ in EARLY + LATE)
        hn, o = carve(area_h, 0, [CP, 2, TPAD])

        x_patch, o = carve(area_a, 0, [128, KP, NPATCH])
        tok_i, o = carve(area_a, o, [VOC, B * NT], I32)
        onehot, o = carve(area_a, o, [VOC, B * NT])
        q_st, k_st, o = [None] * 2, [None] * 2, 0
        for u in range(2):
            q_st[u], o = carve(area_a, o, [128, H, QW], BF16)
            k_st[u], o = carve(area_a, o, [128, H, N], BF16)
        part, o = [None] * 2, 0
        rest = [None] * 2
        for u in range(2):
            part[u], o = carve(area_b, o, [128, 9, BLK], BF16)
            rest[u], o = carve(area_b, o, [128, 3, BLK])
        wd_raw, o = carve(area_c, 0, [128, E * ED])
        wd_1_raw, o = carve(area_c, o, [128, E * ED])
        w1_raw, o = carve(area_c, o, [128, CP])
        w1_1_raw, o = carve(area_c, o, [128, CP])
        h2b, o = carve(area_e, 0, [TT, NTILE, C])
        z = [None] * 2
        for u in range(2):
            z[u], o = carve(area_e, o, [128, 2, BLK])
        xn, o = carve(area_c, 0, [TT, NTILE, C])
        w_tok, _ = carve(area_c, o, [128, KP, C])
        h_block, o = carve(area_c, 2 * E * ED + 2 * CP, [CP, 2, BLK])
        x_block, o = carve(area_c, o, [TT, SUB, C])
        acc, o = carve(area_c, o, [TT, SUB, C])
        y_out = sb("y_out", [TT, SUB, C])
        n_stats = sb("n_stats", [TT, NTILE, 6])
        n_mv = sb("n_mv", [TT, NTILE, 2])
        n_var = sb("n_var", [TT, NTILE])
        n_rstd = sb("n_rstd", [TT, NTILE])

        hn_b = [sb(f"hn_b{u}", [CP, 2, QW]) for u in range(2)]
        v_lo = [sb(f"v_lo{u}", [128, H, 2 * D]) for u in range(2)]
        v_hi = [sb(f"v_hi{u}", [128, H, 2 * D]) for u in range(2)]
        neg_max = [sb(f"neg_max{u}", [128, UNITS]) for u in range(2)]
        e1, att, p_lo, p_hi, o_norm, o = [None] * 2, [None] * 2, [None] * 4, [None] * 4, [None] * 2, 0
        for u in range(2):
            e1[u], o = carve(area_d, o, [128, UNITS, N])
            att[u], o = carve(area_d, o, [128, ATW])
            o_norm[u], o = carve(area_d, o, [128, GROUPS, N])
        for u in range(4):
            p_lo[u], o = carve(area_d, o, [128, T0W])
            p_hi[u], o = carve(area_d, o, [128, N])
        sum1 = [sb(f"sum1_{u}", [128, UNITS]) for u in range(2)]
        rsum1 = [sb(f"rsum1_{u}", [128, UNITS]) for u in range(2)]
        o_raw = [sb(f"o_raw{u}", [128, N]) for u in range(2)]
        rsum2 = sb("rsum2", [128, 2, 4])
        rsum2_rep = sb("rsum2_rep", [128, 2, 4, 2 * D])

        g1 = sb("g1", [CP, BLK])
        logit, shifted, expl, rank, behind, kept, gate = (sb(name, [TT, SUB, E]) for name in
            ("logit", "shifted", "expl", "rank", "behind", "kept", "gate"))
        cmp_ge = sb("cmp_ge", [TT, SUB, E, E])
        top, sum_k, sum_e = (sb(name, [TT, SUB]) for name in ("top", "sum_k", "sum_e"))
        n2_stats = sb("n2_stats", [TT, SUB, 6])
        n2_mv = sb("n2_mv", [TT, SUB, 2])
        n2_var = sb("n2_var", [TT, SUB])
        n2_rstd = sb("n2_rstd", [TT, SUB])
        gate_b = sb("gate_b", [TT, SUB, E])
        stats = sb("stats", [TT, SUB, 6])
        mv = sb("mv", [TT, SUB, 2])
        rstd_y = sb("rstd_y", [TT, SUB])
        vy = sb("vy", [TT, SUB])

        patch_in = [sem(f"patch_in{k}") for k in range(KP)]
        text_in, early_in, late_in = (sem(n) for n in ("text_in", "early_in", "late_in"))
        w_hi_done, w_lo_done = sem("w_hi_done"), sem("w_lo_done")
        x_lo_done = sem("x_lo_done")
        w_up_in = sem("w_up_in")
        shape_in = sem("shape_in")
        compared, ahead_done, route, gate_done, n2_seen, h_block_in = (sem(n) for n in
            ("compared", "ahead_done", "route", "gate_done", "n2_seen", "h_block_in"))
        expert_w_in = sem("expert_w_in")
        preset = sem("preset")
        zeroed = sem("zeroed")
        onehot_done, embed_mm, text_mm, embed_img, embed_txt = (sem(n) for n in
            ("onehot_done", "embed_mm", "text_mm", "embed_img", "embed_txt"))
        h_tp, n_stat, n_mv_done, n_var_done, n_rstd_done, xn_done, xn_tp, hn_done, h2_out, h2b_done = (
            sem(n) for n in ("h_tp", "n_stat", "n_mv_done", "n_var_done", "n_rstd_done", "xn_done", "xn_tp",
                             "hn_done", "h2_out", "h2b_done"))
        qk_mm, part_a, rest_a, part_b, part_c, pad_stored = (sem(n) for n in
            ("qk_mm", "part_a", "rest_a", "part_b", "part_c", "pad_stored"))
        parts_stored = [sem(f"parts_stored{u}") for u in range(2)]
        hnb_in = [sem(f"hnb_in{u}") for u in range(2)]
        stack_in = [sem(f"stack_in{u}") for u in range(2)]
        s_mm_b, s_mm, max_b, max_done, exp1_b, exp1_a, rsum_done, att_done, tr_mm, exp2_done, pv_mm = (sem(n) for n in
            ("s_mm_b", "s_mm", "max_b", "max_done", "exp1_b", "exp1_a", "rsum_done", "att_done", "tr_mm", "exp2_done", "pv_mm"))
        v_mm, v_out, o_out, sum2_tp, rsum2_done, rep_done, rsum2_tp, onorm_done, proj_mm, h_added = (sem(n) for n in
            ("v_mm", "v_out", "o_out", "sum2_tp", "rsum2_done", "rep_done", "rsum2_tp", "onorm_done", "proj_mm", "h_added"))
        g1_mm, g1_done, logit_mm, logit_done, route_dve, route_exp = (sem(n) for n in
            ("g1_mm", "g1_done", "logit_mm", "logit_done", "route_dve", "route_exp"))
        down_mm, z_done, up_mm, acc_done = (sem(n) for n in
            ("down_mm", "z_done", "up_mm", "acc_done"))
        gate_cp, fin_dve, stats_seen, mv_done, vy_done, rstdy_done, y_done, y_stored = (sem(n) for n in
            ("gate_cp", "fin_dve", "stats_seen", "mv_done", "vy_done", "rstdy_done", "y_done", "y_stored"))

        block = ctx.enter_context(nc.Block())
        TXT_BANK = (4, 5, 7)
        NWCHUNK = E * ED // WCHUNK
        IMG_BLKS, IMG_N = 2, NPATCH // 2
        TXT_BLKS, TXT_B = 4, 4

        def router_bank(n):
            return 0 if isinstance(n, int) and n == 0 else 2

        def batches_before(tokens):
            return -(-tokens // N)

        TEXT_DMAS = 1 + 2 + 4 * (1 + 1) + 2
        LATE_DMAS = 4

        @block.sync
        def _(sp):
            def load(dst, src, s):
                sp.dma_start(dst, src).then_inc(s, 16)

            for k in range(KP):
                load(w_tok[:, k, :], a["w_tok"][:, k, :], patch_in[k])
                load(x_patch[:, k, :], a["x_patch"][:, k, :], patch_in[k])
            load(early[:], a["early"], early_in)
            load(tok_i, a["tokens"].partition_broadcast(VOC), text_in)
            load(iota[:], a["iota"], text_in)
            load(b_tok[:], a["b_tok"], text_in)
            for i in range(4):
                load(table[16 * i:16 * i + 16, 0:64], a["color"][i, :].partition_broadcast(16), text_in)
                load(table[i:64:4, 128:C], a["quantity"][i, :].partition_broadcast(16), text_in)
            load(table[64:VOC, :], a["special"], text_in)
            load(pe_sb[:], a["pe"], text_in)
            load(late[:], a["late"], late_in)
            load(b2[:], a["b2"].partition_broadcast(TT), late_in)
            load(gamma[:], a["gamma"].partition_broadcast(TT), late_in)
            load(beta[:], a["beta"].partition_broadcast(TT), late_in)

            sp.wait_ge(preset, 1)
            for t in range(9):
                load(parts_dram[t // 3, 128 * (t % 3):128 * (t % 3) + 128, T:TPAD], zero[:], pad_stored)

            def stacks(u, tok, slots=range(8)):
                for s in slots:
                    rows = slice(16 * s, 16 * s + 16)
                    load(q_st[u][rows], parts_dram[Q_PART[s], 0:C, bass.ds(tok, QW)]
                         .rearrange("(h d) n -> d h n", d=D), stack_in[u])
                    load(k_st[u][rows], parts_dram[K_PART[s], C:2 * C, bass.ds(tok, N)]
                         .rearrange("(h d) n -> d h n", d=D), stack_in[u])

            for n in range(NBLK):
                sp.wait_ge(part_c, 3 * n + 3)
                for k in range(3):
                    load(parts_dram[k, :, n * BLK:(n + 1) * BLK].rearrange("(t p) n -> p t n", p=128),
                         part[n % 2][:, 3 * k:3 * k + 3, :], parts_stored[n % 2])
                if n == 1:
                    sp.wait_ge(parts_stored[0], 48)
                if 1 <= n < 4:
                    stacks(0, 0, range(3 * n - 3, min(3 * n, 8)))
                if n in (1, 2):
                    load(hn_b[n - 1][:], hn[:, :, (n - 1) * N:(n - 1) * N + QW], hnb_in[n - 1])
            stacks(1, N)

            for u in range(2):
                sp.wait_ge(parts_stored[u], 48 * NBLK // 2)
            sp.wait_ge(pad_stored, 16 * 9)
            sp.wait_ge(hn_done, NBLK)
            sp.wait_ge(xn_tp, NBLK)

            def weights(chunk):
                cols = bass.ds(chunk * WCHUNK, WCHUNK)
                for dst, name in ((wd_raw, "wd_0"), (wd_1_raw[0:F1], "wd_1"), (wd_1_raw[F1:], "wd_1")):
                    load(dst[:, cols], a[name][:, cols], expert_w_in)

            def loads(it, first, last):
                if first:
                    return
                weights(it - 1)
                if last:
                    weights(it)
                    for dst, name in ((w1_raw, "w1_0"), (w1_1_raw[0:F1], "w1_1"), (w1_1_raw[F1:], "w1_1")):
                        load(dst, a[name], expert_w_in)
                for u in range(2):
                    tok = it * (2 * N) + u * N
                    wait(sp, v_mm, 2 * it + u - 1)
                    wait(sp, s_mm, PER * it + PAIRS * (u - 1))
                    load(hn_b[u][:], hn[:, :, bass.ds(tok, QW)], hnb_in[u])
                    stacks(u, tok)

            looped(sp, loads)
            load(w_up[:], a["w_up"], w_up_in)

            out_v = out.rearrange("(t p) c -> p t c", p=TT)
            sp.wait_ge(h_added, batches_before(BLK))
            load(h_block, hT[:, :, 0:BLK], h_block_in)

            def stores(i, first, last_block):
                for half in range(2):
                    sp.wait_ge(y_done, 2 * i + half + 1)
                    load(out_v[:, bass.ds(i * SUB + 2 * half, 2), :], y_out[:, 2 * half:2 * half + 2, :], y_stored)

            block_loop(sp, stores)
            sp.wait_ge(y_stored, 32 * NBLK)

        @block.tensor
        def _(pe):
            mm, tp = nc.tensor.matmul, nc.tensor.transpose

            def embed_images():
                for k in range(KP):
                    pe.wait_ge(patch_in[k], 32)
                    for i in range(IMG_BLKS):
                        for m in range(2):
                            last = mm(bank[2 * i + m][0:CP, 0:IMG_N], w_tok[:, k, CP * m:CP * m + CP],
                                      x_patch[:, k, IMG_N * i:IMG_N * (i + 1)], start=(k == 0), stop=(k == KP - 1))
                            if k == KP - 1:
                                last.then_inc(embed_mm, 1)

            def embed_text(i):
                pe.wait_ge(shape_in, 16 * 16)
                pe.wait_ge(onehot_done, i + 1)
                for m in range(2):
                    q = 2 * i + m
                    if q >= 3:
                        pe.wait_ge(embed_txt, q - 2)
                    mm(bank[TXT_BANK[q % 3]][0:CP, 0:512], table[:, CP * m:CP * m + CP],
                       onehot[:, 512 * i:512 * i + 512], start=True, stop=True).then_inc(text_mm, 1)

            def to_tokens(h, banks):
                for s in range(SUB):
                    for c in range(2):
                        last = tp(bank[banks + s // 2][0:TT, C * (s % 2) + CP * c:][:, 0:CP],
                                  h[:, c, TT * s:TT * s + TT], ident[0:CP, 0:CP])
                last.then_inc(h_tp, 1)

            def to_features(x, banks, chunks):
                for s in range(SUB):
                    for c, lo, hi in chunks:
                        last = tp(bank[banks + c][0:hi - lo, TT * s:TT * s + TT],
                                  x[:, s, lo:hi], ident[0:TT, 0:TT])
                last.then_inc(xn_tp, 1)

            def norm_in(n):
                batches = batches_before((n + 1) * BLK)
                pe.wait_ge(embed_img, 2 * -(-batches // 8))
                pe.wait_ge(embed_txt, 2 * -(-batches // TXT_B))
                if n < 2:
                    pe.wait_ge(embed_img, 2 * n + 2)
                if n >= 2:
                    pe.wait_ge(hn_done, n - 1)
                to_tokens(hT[:, :, n * BLK:(n + 1) * BLK], 2 * (n % 2))

            def norm_out(n):
                pe.wait_ge(xn_done, n + 1)
                to_features(xn[:, SUB * n:SUB * (n + 1), :], 2 * (n % 2), ((0, 0, CP), (1, CP, C)))

            embed_images()
            embed_text(0)
            embed_text(1)
            pe.wait_ge(early_in, 16)
            norm_in(0)
            embed_text(2)
            embed_text(3)
            norm_in(1)
            for n in range(NBLK + 1):
                if n < NBLK:
                    norm_out(n)
                if n >= 1:
                    pe.wait_ge(hn_done, n)
                    for t in range(3):
                        q = 3 * (n - 1) + t
                        if q >= 3:
                            pe.wait_ge(rest_a, q - 2)
                        for c in range(2):
                            last = mm(bank[4 + t][:, 0:BLK], w_qk[:, c, 128 * t:128 * t + 128],
                                      hn[:, c, (n - 1) * BLK:n * BLK], start=(c == 0), stop=(c == 1))
                        last.then_inc(qk_mm, 1)
                if n + 2 < NBLK:
                    norm_in(n + 2)
            pe.wait_ge(late_in, 16 * LATE_DMAS)
            pe.wait_ge(rest_a, 3 * NBLK)

            def split_products(dst, cols, w_hi, w_lo, w_1, tokens):
                pairs = ((w_hi, x_hi), (w_lo, x_hi), (w_hi, x_lo), (w_1, x1_hi), (w_1, x1_lo))
                for n, (w, x) in enumerate(pairs):
                    last = mm(dst, w[:, cols], x[:, tokens], start=(n == 0), stop=(n == len(pairs) - 1))
                return last

            def second_norm_in(n):
                pe.wait_ge(h_block_in, 16 * n + 16)
                wait(pe, g1_done, n)
                wait(pe, logit_done, n)
                if isinstance(n, int) and n == 0:
                    pe.wait_ge(exp1_a, NPAIR)
                to_tokens(h_block, router_bank(n))

            def second_norm_out(n):
                pe.wait_ge(xn_done, NBLK + n + 1)
                pe.wait_ge(h2_out, n + 1)
                to_features(x_block, router_bank(n), ((0, 0, F0), (1, F1, C), (1, F0, C)))

            def router_hidden(n):
                if isinstance(n, int) and n == 0:
                    pe.wait_ge(w_lo_done, 2 * NWCHUNK + 2)
                pe.wait_ge(hn_done, NBLK + n + 1)
                pe.wait_ge(x_lo_done, n + 1)
                split_products(bank[router_bank(n)][0:CP, 0:BLK], slice(0, CP), w1_hi, w1_lo, w1_1,
                               bass.ds(n * BLK, BLK)).then_inc(g1_mm, 1)

            def router_logits(n):
                pe.wait_ge(g1_done, n + 1)
                for s in range(SUB):
                    last = mm(bank[router_bank(n) + 1][0:TT, E * s:E * s + E], g1[:, TT * s:TT * s + TT], w2, start=True, stop=True)
                last.then_inc(logit_mm, 1)

            def attention(it, first, last_it):
                def live(k, unit=1):
                    return (not first or k >= 0) and (not last_it or k < PER // unit)

                def scores(k):
                    h, u = 2 * (k % PAIRS), k // PAIRS % 2
                    if k % PAIRS == 0:
                        pe.wait_ge(stack_in[u], it * 256 + 256 * (k // PAIRS // 2 + 1))
                    wait(pe, exp1_b, PER * it + k)
                    for e in range(2):
                        last = mm(bank[2][64 * e:64 * e + 64, 0:N], q_st[u][:, h + e, 128:QW],
                                  k_st[u][:, h + e, :], start=True, stop=True)
                    last.then_inc(s_mm_b, 1)
                    wait(pe, exp1_a, PER * it + k - 1)
                    o = bank[k % 2]
                    mm(o[:, 0:N], q_st[u][:, h, 0:128], k_st[u][:, h, :], start=True, stop=True)
                    mm(o[:, N:N + REST], q_st[u][:, h + 1, 0:128], k_st[u][:, h + 1, 128:N], start=True, stop=True)
                    mm(o[:, N + REST:2 * N], q_st[u][:, h + 1, 0:128], k_st[u][:, h + 1, 0:128],
                       start=True, stop=True).then_inc(s_mm, 1)

                def transposes(k):
                    pe.wait_ge(att_done, PER * it + k + 1)
                    wait(pe, exp2_done, PER * it + k)
                    t = att[k % 2]
                    rest_ = t[:, AT2:AT2 + 192]
                    tp(bank[3][:, 0:128], t[:, 0:128], ident[:])
                    tp(bank[3][:, 128:128 + PW], rest_[0:PW, 0:128], ident[0:PW, 0:PW])
                    tp(bank[3][:, 128 + PW:T0W], t[:, AT1 + REST:AT1 + N], ident[:])
                    tp(bank[4][:, 64:N], rest_[0:PW, 64:192], ident[0:PW, 0:PW])
                    tp(bank[4][0:64, 128:128 + PW], rest_[0:PW, 128:192], ident[0:PW, 0:PW])
                    tp(bank[4][:, 0:128], t[:, 128:256], ident[:]).then_inc(tr_mm, 1)

                def values(g):
                    b, u = g // GROUPS, g // GROUPS % 2
                    pe.wait_ge(exp2_done, PER * it + 2 * g + 2)
                    wait(pe, o_out, PER // 2 * it + g)
                    if g % GROUPS == 0:
                        pe.wait_ge(v_out, 2 * it + b + 1)
                    p = [(2 * g + pair) % 4 for pair in range(2)]
                    parts = ([(j, slice(0, N), 0) if j % 2 == 0 else (j, slice(0, 128), 128 + PW) for j in range(4)]
                             + [(j, slice(128, N), 192) for j in (1, 3)])
                    for n, (j, dst, at) in enumerate(parts):
                        mm(bank[5][32 * j:32 * j + 32, dst], v_lo[u][:, 4 * (g % GROUPS) + j, :],
                           p_lo[p[j // 2]][:, at:at + dst.stop - dst.start], start=(n < 4), stop=False)
                    for n, (j, dst, at) in enumerate(parts):
                        last = mm(bank[5][32 * j:32 * j + 32, dst], v_hi[u][:, 4 * (g % GROUPS) + j, :],
                                  p_hi[p[j // 2]][:, dst], start=False, stop=(j % 2 == 0 or n >= 4))
                    last.then_inc(pv_mm, 1)

                def sums(g):
                    pe.wait_ge(o_out, PER // 2 * it + g + 1)
                    wait(pe, onorm_done, PER // 2 * it + g)
                    tp(bank[6][:, 0:128], o_raw[g % 2][:, 0:128], ident[:])
                    tp(bank[6][0:REST, 128:256], o_raw[g % 2][:, 128:N], ident[:]).then_inc(sum2_tp, 1)

                def sums_back(g):
                    pe.wait_ge(rep_done, PER // 2 * it + g + 1)
                    rep = rsum2_rep[:].rearrange("p c j d -> p c (j d)")
                    tp(bank[6][:, 256:384], rep[:, 0, :], ident[:])
                    tp(bank[6][:, 384:384 + REST], rep[0:REST, 1, :], ident[0:REST, 0:REST]).then_inc(rsum2_tp, 1)

                def v_proj(b):
                    u = b % 2
                    pe.wait_ge(hnb_in[u], it * 16 + 16 * (b // 2) + 16)
                    wait(pe, h_added, 2 * it + b - 1)
                    halves = w_v[:, :, :].rearrange("p c (i e d) -> p c e i d", e=2, d=D)
                    for c in range(2):
                        mm(bank[7][:, 0:C], hn_b[u][:, c, 0:128], w_v[:, c, :], start=(c == 0), stop=(c == 1))
                    for e in range(2):
                        for c in range(2):
                            last = mm(bank[7][64 * e:64 * e + 64, C:C + CP], hn_b[u][:, c, 128:QW],
                                      halves[:, c, e], start=(c == 0), stop=(c == 1))
                    last.then_inc(v_mm, 1)

                def out_proj(b, half):
                    if half == 0:
                        pe.wait_ge(v_out, 2 * it + (min(b + 2, 2) if last_it else b + 2))
                    pe.wait_ge(onorm_done, PER // 2 * it + GROUPS * b + 2 + half)
                    for g, m in ((0, 0), (0, 1), (1, 0), (1, 1), (2, 0), (2, 1))[3 * half:3 * half + 3]:
                        last = mm(bank[7][0:CP, N * m:N * m + N], w_o[:, g, CP * m:CP * m + CP],
                                  o_norm[b % 2][:, g, :], start=(g == 0 and m == 0), stop=(g == 2 and m == 1))
                    if half == 1:
                        last.then_inc(proj_mm, 1)

                for s in pair_steps(first, last_it):
                    if live(s + 2):
                        scores(s + 2)
                    if live(s):
                        transposes(s)
                    if s % 2 == 0 and live((s - 2) // 2, 2):
                        values((s - 2) // 2)
                    if s % 2 == 1 and live((s - 3) // 2, 2):
                        sums((s - 3) // 2)
                    if s % 2 == 0 and live((s - 4) // 2, 2):
                        sums_back((s - 4) // 2)
                    if s % PAIRS == 5 and live((s + 1) // PAIRS, PAIRS):
                        v_proj((s + 1) // PAIRS)
                    if s % PAIRS == 1 and live((s - 7) // PAIRS, PAIRS):
                        out_proj((s - 7) // PAIRS, 0)
                    if s % PAIRS == 3 and live((s - 9) // PAIRS, PAIRS):
                        if last_it and s > PER:
                            router_hidden(0)
                        out_proj((s - 9) // PAIRS, 1)
                    if last_it and s == PER - 1:
                        second_norm_in(0)
                    if last_it and s == PER + 1:
                        second_norm_out(0)

            looped(pe, attention)

            router_logits(0)
            pe.wait_ge(w_up_in, 16)

            def experts(i, first, last_block):
                def down(e):
                    for half in range(2):
                        q = 2 * e + half
                        if first and q == 1:
                            pe.wait_ge(logit_done, 1)
                        if not (first and q < 2):
                            pe.wait_ge(z_done, 2 * E * i + q - 1)
                        at = ED * e + 128 * half
                        split_products(bank[half][:, 0:BLK], slice(at, at + 128), wd_hi, wd_lo, wd_1,
                                       bass.ds(i * BLK, BLK)).then_inc(down_mm, 1)

                def up(e):
                    pe.wait_ge(z_done, 2 * E * i + 2 * e + 2)
                    if not (first and e < 2):
                        pe.wait_ge(acc_done, E * i + e - 1)
                    for s in range(SUB):
                        for half in range(2):
                            last = mm(bank[4 + 2 * (e % 2) + s // 2][0:TT, C * (s % 2):C * (s % 2) + C],
                                      z[e % 2][:, half, TT * s:TT * s + TT], w_up[:, 2 * e + half, :],
                                      start=(half == 0), stop=(half == 1))
                        if s % 2 == 1:
                            last.then_inc(up_mm, 1)

                between = {} if last_block else {0: second_norm_in, 2: second_norm_out, 4: router_hidden,
                                                 6: router_logits}
                down(0)
                for e in range(E):
                    if e + 1 < E:
                        down(e + 1)
                    if e in between:
                        between[e](i + 1)
                    up(e)

            block_loop(pe, experts)

        @block.scalar
        def _(act):
            fn = nc.scalar.activation
            act.wait_ge(text_in, 16 * TEXT_DMAS)
            for i in range(IMG_BLKS):
                for m in range(2):
                    act.wait_ge(embed_mm, 2 * i + m + 1)
                    dst = hT[:, m, i * 8 * N:(i + 1) * 8 * N].rearrange("p (b n) -> p b n", n=N)[:, :, 0:NI]
                    fn(dst, bank[2 * i + m][0:CP, 0:IMG_N].rearrange("p (b n) -> p b n", n=NI), ACT.Identity,
                       bias=b_tok[:, m:m + 1]).then_inc(embed_img, 1)

            act.wait_ge(early_in, 16)
            for n in range(NBLK + 1):
                if n < NBLK:
                    act.wait_ge(xn_tp, n + 1)
                    for c in range(2):
                        ins = fn(hn[:, c, n * BLK:(n + 1) * BLK], bank[2 * (n % 2) + c][0:CP, 0:BLK], ACT.Copy)
                    ins.then_inc(hn_done, 1)
                if n >= 1:
                    u = (n - 1) % 2
                    if n >= 3:
                        act.wait_ge(parts_stored[u], 48 * ((n - 1) // 2))
                    for t in range(4):
                        q = 3 * (n - 1) + t
                        if t < 3:
                            act.wait_ge(qk_mm, q + 1)
                            fn(part[u][:, t, :], bank[4 + t][:, 0:BLK], ACT.Copy,
                               scale=qk_scale[:, t:t + 1]).then_inc(part_a, 1)
                        if t >= 1:
                            act.wait_ge(rest_a, q)
                            fn(part[u][:, 2 + t, :], rest[u][:, t - 1, :], ACT.Copy).then_inc(part_b, 1)

            def residual(n):
                act.wait_ge(n_stat, NBLK + n + 1)
                for s in range(0, SUB, 2):
                    ins = fn(h2b[:, bass.ds(n * SUB + s, 2), :], bank[router_bank(n) + s // 2][0:TT, 0:2 * C], ACT.Copy)
                ins.then_inc(h2_out, 1)

            def attention(it, first, last_it):
                def live(k, unit=1):
                    return (not first or k >= 0) and (not last_it or k < PER // unit)

                def exp1(k, units):
                    src = [bank[k % 2][:, 0:N], bank[k % 2][:, N:2 * N], bank[2][:, 0:N]]
                    for w in units:
                        ins = fn(e1[k % 2][:, w, :], src[w], ACT.Exp, bias=neg_max[k % 2][:, w:w + 1],
                                 accum_out=sum1[k % 2][:, w:w + 1])
                    return ins

                def exp2(k):
                    act.wait_ge(tr_mm, PER * it + k + 1)
                    wait(act, pv_mm, PER // 2 * it + k // 2 - 1)
                    fn(p_lo[k % 4][:], bank[3][:, 0:T0W], ACT.Exp)
                    fn(p_hi[k % 4][:], bank[4][:, 0:N], ACT.Exp).then_inc(exp2_done, 1)

                def out_raw(g):
                    act.wait_ge(pv_mm, PER // 2 * it + g + 1)
                    wait(act, onorm_done, PER // 2 * it + g - 1)
                    fn(o_raw[g % 2][:], bank[5][:, 0:N], ACT.Copy).then_inc(o_out, 1)

                def v_copy(b):
                    act.wait_ge(v_mm, 2 * it + b + 1)
                    fn(v_lo[b % 2][:, :, 0:D], bank[7][:, 0:C].rearrange("p (h d) -> p h d", d=D), ACT.Copy)
                    for e in range(2):
                        rows = slice(64 * e, 64 * e + REST)
                        ins = fn(v_hi[b % 2][rows, e::2, 0:D],
                                 bank[7][rows, C:C + CP].rearrange("p (h d) -> p h d", d=D), ACT.Copy)
                    ins.then_inc(v_out, 1)

                for s in pair_steps(first, last_it):
                    if last_it and s == PER:
                        residual(0)
                    if s % 2 == 1 and live((s - 3) // 2, 2):
                        out_raw((s - 3) // 2)
                    if s % PAIRS == 0 and live(s // PAIRS, PAIRS):
                        v_copy(s // PAIRS)
                    if live(s + 2):
                        act.wait_ge(max_b, PER * it + s + 3)
                        exp1(s + 2, (2,)).then_inc(exp1_b, 1)
                    if live(s):
                        exp2(s)
                    if live(s + 2):
                        act.wait_ge(max_done, PER * it + s + 3)
                        exp1(s + 2, (0, 1)).then_inc(exp1_a, 1)

            looped(act, attention)

            def rounded(n):
                act.wait_ge(xn_tp, NBLK + n + 1)
                for c, dst in enumerate((x_hi, x1_hi)):
                    ins = fn(dst[:, bass.ds(n * BLK, BLK)], bank[router_bank(n) + c][:, 0:BLK], ACT.Copy)
                ins.then_inc(hn_done, 1)

            def hidden(n):
                act.wait_ge(g1_mm, n + 1)
                fn(g1[:], bank[router_bank(n)][0:CP, 0:BLK], ACT.Gelu, bias=b1).then_inc(g1_done, 1)

            def load_block(n):
                act.wait_ge(h_tp, NBLK + n)
                act.dma_start(h_block, hT[:, :, bass.ds(n * BLK, BLK)]).then_inc(h_block_in, 16)

            for u in range(2):
                act.wait_ge(hnb_in[u], 16 * B // 2)
            for step in (rounded, hidden):
                step(0)

            def experts(i, first, last_block):
                between = {} if last_block else {1: residual, 3: rounded, 5: hidden}
                if first:
                    act.wait_ge(h_added, B)
                if not last_block:
                    load_block(i + 1)
                for e in range(E):
                    for half in range(2):
                        act.wait_ge(down_mm, 2 * E * i + 2 * e + half + 1)
                        if half == 0 and not (first and e < 2):
                            act.wait_ge(up_mm, 2 * E * i + 2 * e - 2)
                        fn(z[e % 2][:, half, :], bank[half][:, 0:BLK], ACT.Gelu,
                           bias=down_b[:, 2 * e + half:2 * e + half + 1]).then_inc(z_done, 1)
                    if e in between:
                        between[e](i + 1)

            block_loop(act, experts)

        @block.vector
        def _(dve):
            v = nc.vector
            v.memset(hn[:, :, T:TPAD], 0.0)
            v.memset(one[:], 1.0)
            for u in range(2):
                v.memset(v_lo[u][:], 1.0)
                v.memset(v_hi[u][:], 0.0)
                v.memset(att[u][:], 0.0)
            v.memset(bank[6][:], 1.0).then_inc(zeroed, 1)
            dve.wait_ge(zeroed, 1)
            for u in range(2):
                for e in range(2):
                    v.memset(v_hi[u][64 * e:64 * e + REST, e::2, D:2 * D], 1.0)
            v.memset(zero[:], 0.0).then_inc(preset, 1)

            dve.wait_ge(text_in, 16 * TEXT_DMAS)
            for i in range(TXT_BLKS):
                cols = slice(512 * i, 512 * i + 512)
                v.tensor_scalar(onehot[:, cols], tok_i[:, cols], float(VOC - 1), iota[:, 0:1], ALU.min, ALU.is_equal)\
                    .then_inc(onehot_done, 1)
            def embed_text(i):
                for m in range(2):
                    q = 2 * i + m
                    dve.wait_ge(text_mm, q + 1)
                    dst = hT[:, m, i * TXT_B * N:(i + 1) * TXT_B * N].rearrange("p (b n) -> p b n", n=N)[:, :, NI:N]
                    v.scalar_tensor_tensor(
                        out=dst, in0=bank[TXT_BANK[q % 3]][0:CP, :].rearrange("p (b n) -> p b n", n=NT),
                        scalar=float(C) ** 0.5, in1=pe_sb[:, m, :].unsqueeze(1).to_broadcast([CP, TXT_B, NT]),
                        op0=ALU.mult, op1=ALU.add).then_inc(embed_txt, 1)

            def statistics(n):
                t0 = SUB * n
                dve.wait_ge(h_tp, n + 1)
                for s in range(SUB):
                    ins = v.bn_stats(n_stats[:, t0 + s, :],
                                     bank[2 * (n % 2) + s // 2][0:TT, C * (s % 2):C * (s % 2) + C])
                ins.then_inc(n_stat, 1)
                dve.wait_ge(n_stat, n + 1)
                for s in range(SUB):
                    ins = v.bn_aggr(n_mv[:, t0 + s, :], n_stats[:, t0 + s, :])
                ins.then_inc(n_mv_done, 1)

            def normalised(n):
                dve.wait_ge(n_rstd_done, n + 1)
                for s in range(SUB):
                    t = SUB * n + s
                    ins = v.tensor_scalar(xn[:, t, :], bank[2 * (n % 2) + s // 2][0:TT, C * (s % 2):C * (s % 2) + C],
                                          n_mv[:, t, 0:1], n_rstd[:, t:t + 1], ALU.subtract, ALU.mult)
                ins.then_inc(xn_done, 1)

            embed_text(0)
            embed_text(1)
            dve.wait_ge(early_in, 16)
            statistics(0)
            embed_text(2)
            normalised(0)
            embed_text(3)
            for n in range(NBLK + 1):
                if n + 1 < NBLK:
                    statistics(n + 1)
                    normalised(n + 1)
                if n >= 1:
                    u = (n - 1) % 2
                    for t in range(3):
                        dve.wait_ge(part_a, 3 * (n - 1) + t + 1)
                        if n >= 3 and t == 0:
                            dve.wait_ge(part_c, 3 * (n - 2))
                        v.scalar_tensor_tensor(
                            out=rest[u][:, t, :], in0=bank[4 + t][:, 0:BLK], scalar=qk_scale[:, t:t + 1],
                            in1=part[u][:, t, :], op0=ALU.mult, op1=ALU.subtract).then_inc(rest_a, 1)
            dve.wait_ge(late_in, 16 * LATE_DMAS)

            def second_statistics(n):
                dve.wait_ge(h_tp, NBLK + n + 1)
                for s in range(SUB):
                    ins = v.bn_stats(n2_stats[:, s, :], bank[router_bank(n) + s // 2][0:TT, C * (s % 2):C * (s % 2) + C])
                ins.then_inc(n_stat, 1)
                dve.wait_ge(n_stat, NBLK + n + 1)
                dve.sem_inc(n2_seen, 1)
                for s in range(SUB):
                    ins = v.bn_aggr(n2_mv[:, s, :], n2_stats[:, s, :])
                ins.then_inc(n_mv_done, 1)

            def second_normalised(n):
                dve.wait_ge(n_rstd_done, NBLK + n + 1)
                dve.wait_ge(h2_out, n + 1)
                wait(dve, acc_done, E * (n - 1) + 1)
                for s in range(SUB):
                    ins = v.tensor_scalar(x_block[:, s, :],
                                          bank[router_bank(n) + s // 2][0:TT, C * (s % 2):C * (s % 2) + C],
                                          n2_mv[:, s, 0:1], n2_rstd[:, s:s + 1], ALU.subtract, ALU.mult)
                ins.then_inc(xn_done, 1)

            def second_parts(n):
                dve.wait_ge(hn_done, NBLK + n + 1)
                for c, (lo, hi) in enumerate(((x_lo, x_hi), (x1_lo, x1_hi))):
                    ins = v.tensor_tensor(lo[:, bass.ds(n * BLK, BLK)], bank[router_bank(n) + c][:, 0:BLK],
                                          hi[:, bass.ds(n * BLK, BLK)].bitcast(F32), ALU.subtract)
                ins.then_inc(x_lo_done, 1)

            def attention(it, first, last_it):
                def live(k, unit=1):
                    return (not first or k >= 0) and (not last_it or k < PER // unit)

                def maxima_rest(k):
                    dve.wait_ge(s_mm_b, PER * it + k + 1)
                    v.tensor_reduce(neg_max[k % 2][:, 2:3], bank[2][:, 0:N], AX_X, ALU.max, negate=True)\
                        .then_inc(max_b, 1)

                def maxima(k):
                    dve.wait_ge(s_mm, PER * it + k + 1)
                    v.tensor_reduce(neg_max[k % 2][:, 0:2], bank[k % 2][:, 0:2 * N].rearrange("p (e n) -> p e n", e=2),
                                    AX_X, ALU.max, negate=True).then_inc(max_done, 1)

                def rsum(k):
                    dve.wait_ge(exp1_a, PER * it + k + 1)
                    v.reciprocal(rsum1[k % 2][:], sum1[k % 2][:]).then_inc(rsum_done, 1)

                def normalise(k):
                    wait(dve, tr_mm, PER * it + k - 1)
                    dve.wait_ge(rsum_done, PER * it + k + 1)
                    for w, (at, mask) in enumerate(((0, mask_a), (AT1, mask_r), (AT2, mask_b))):
                        ins = v.scalar_tensor_tensor(
                            out=att[k % 2][:, at:at + N], in0=e1[k % 2][:, w, :],
                            scalar=rsum1[k % 2][:, w:w + 1], in1=mask[:], op0=ALU.mult, op1=ALU.mult)
                    ins.then_inc(att_done, 1)

                def reciprocals(g):
                    dve.wait_ge(sum2_tp, PER // 2 * it + g + 1)
                    wait(dve, rep_done, PER // 2 * it + g)
                    sums = bank[6][:, 0:256].rearrange("p (c j d) -> p c j d", c=2, j=4)[:, :, :, D]
                    v.reciprocal(rsum2[:], sums).then_inc(rsum2_done, 1)

                def scale_out(g):
                    dve.wait_ge(rsum2_tp, PER // 2 * it + g + 1)
                    v.tensor_tensor(o_norm[g // GROUPS % 2][:, g % GROUPS, :], o_raw[g % 2][:],
                                    bank[6][:, 256:256 + N], ALU.mult).then_inc(onorm_done, 1)

                def add_out(b):
                    dve.wait_ge(proj_mm, 2 * it + b + 1)
                    for m in range(2):
                        h = hT[:, m, bass.ds(it * (2 * N) + b * N, N)]
                        ins = v.scalar_tensor_tensor(out=h, in0=bank[7][0:CP, N * m:N * m + N],
                                                     scalar=b_o[:, m:m + 1], in1=h, op0=ALU.add, op1=ALU.add)
                    ins.then_inc(h_added, 1)

                for s in pair_steps(first, last_it):
                    if s % 2 == 1 and live((s - 5) // 2, 2):
                        scale_out((s - 5) // 2)
                    if s % 2 == 0 and live((s - 4) // 2, 2):
                        reciprocals((s - 4) // 2)
                    if last_it and s == PER:
                        second_statistics(0)
                    if last_it and s == PER + 1:
                        second_normalised(0)
                    if last_it and s == PER + 3:
                        second_parts(0)
                    if live(s + 2):
                        maxima_rest(s + 2)
                    if live(s + 1):
                        rsum(s + 1)
                    if live(s + 2):
                        maxima(s + 2)
                    if live(s + 1):
                        normalise(s + 1)
                    if s % PAIRS == 4 and live((s - 10) // PAIRS, PAIRS):
                        add_out((s - 10) // PAIRS)

            looped(dve, attention)

            ROUTE = 9

            def logits(n):
                dve.wait_ge(logit_mm, n + 1)
                v.tensor_tensor(logit[:], bank[router_bank(n) + 1][0:TT, 0:SUB * E].rearrange("p (s e) -> p s e", e=E),
                                b2[:].unsqueeze(1).to_broadcast([TT, SUB, E]), ALU.add).then_inc(logit_done, 1)
                dve.wait_ge(logit_done, n + 1)
                v.tensor_reduce(top[:], logit[:], AX_X, ALU.max).then_inc(route, 1)
                v.tensor_tensor(cmp_ge[:], logit[:].unsqueeze(2).to_broadcast([TT, SUB, E, E]),
                                logit[:].unsqueeze(3).to_broadcast([TT, SUB, E, E]), ALU.is_ge).then_inc(compared, 1)
                dve.wait_ge(route, ROUTE * n + 1)
                v.tensor_tensor(shifted[:], logit[:], top[:].unsqueeze(2).to_broadcast([TT, SUB, E]),
                                ALU.subtract).then_inc(route_dve, 1)

            def ranks(n):
                dve.wait_ge(ahead_done, n + 1)
                v.tensor_reduce(rank[:], cmp_ge[:], AX_X, ALU.add).then_inc(route, 1)
                v.tensor_reduce(behind[:], cmp_ge[:].rearrange("p t e j -> p t j e"), AX_X, ALU.add)\
                    .then_inc(route, 1)
                dve.wait_ge(route, ROUTE * n + 3)
                v.tensor_tensor(rank[:], rank[:], behind[:], ALU.subtract).then_inc(route, 1)
                dve.wait_ge(route, ROUTE * n + 4)
                v.tensor_tensor(rank[:], rank[:], later.unsqueeze(1).to_broadcast([TT, SUB, E]), ALU.add)\
                    .then_inc(route, 1)

            def gates(n):
                flat = (t[:].rearrange("p t e -> p (t e)") for t in (kept, rank, expl))
                kept_, rank_, expl_ = flat
                dve.wait_ge(route_exp, n + 1)
                v.tensor_reduce(sum_e[:], expl[:], AX_X, ALU.add)
                dve.wait_ge(route, ROUTE * n + 5)
                v.scalar_tensor_tensor(out=kept_, in0=rank_, scalar=1.5, in1=expl_, op0=ALU.is_lt, op1=ALU.mult)\
                    .then_inc(route, 1)
                dve.wait_ge(route, ROUTE * n + 6)
                v.tensor_reduce(sum_k[:], kept[:], AX_X, ALU.add).then_inc(route, 1)
                dve.wait_ge(route, ROUTE * n + 7)
                v.scalar_tensor_tensor(out=sum_k[:], in0=sum_e[:], scalar=GATE_EPS, in1=sum_k[:],
                                       op0=ALU.mult, op1=ALU.add).then_inc(route, 1)
                dve.wait_ge(route, ROUTE * n + 8)
                v.reciprocal(sum_e[:], sum_k[:]).then_inc(route, 1)
                dve.wait_ge(route, ROUTE * n + 9)
                v.tensor_tensor(gate[:], kept[:], sum_e[:].unsqueeze(2).to_broadcast([TT, SUB, E]),
                                ALU.mult).then_inc(gate_done, 1)

            for step in (logits, ranks, gates):
                step(0)

            def experts(i, first, last_block):
                between = {} if last_block else {0: second_statistics, 1: second_normalised, 3: second_parts,
                                                 6: logits, 7: ranks}
                dve.wait_ge(gate_done, i + 1)
                v.tensor_copy(gate_b[:], gate[:]).then_inc(gate_cp, 1)
                for e in range(E):
                    if e in between:
                        between[e](i + 1)
                    if e == 0:
                        wait(dve, y_done, 2 * i)
                        dve.wait_ge(gate_cp, i + 1)
                    wait(dve, acc_done, E * i + e)
                    for s in range(SUB):
                        if s % 2 == 0:
                            dve.wait_ge(up_mm, 2 * E * i + 2 * e + 1 + s // 2)
                        before = acc[:, s, :] if e else x_block[:, s, :]
                        ins = v.scalar_tensor_tensor(
                            out=acc[:, s, :], in0=bank[4 + 2 * (e % 2) + s // 2][0:TT, C * (s % 2):C * (s % 2) + C],
                            scalar=gate_b[:, s, e:e + 1], in1=before, op0=ALU.mult, op1=ALU.add)
                    ins.then_inc(acc_done, 1)
                if not last_block:
                    gates(i + 1)
                dve.wait_ge(acc_done, E * i + E)
                for s in range(SUB):
                    ins = v.bn_stats(stats[:, s, :], acc[:, s, :])
                ins.then_inc(fin_dve, 1)
                dve.wait_ge(fin_dve, 2 * i + 1)
                dve.sem_inc(stats_seen, 1)
                for s in range(SUB):
                    ins = v.bn_aggr(mv[:, s, :], stats[:, s, :])
                ins.then_inc(mv_done, 1)
                dve.wait_ge(mv_done, i + 1)
                for s in range(SUB):
                    ins = v.scalar_tensor_tensor(out=acc[:, s, :], in0=acc[:, s, :], scalar=mv[:, s, 0:1],
                                                 in1=gamma[:], op0=ALU.subtract, op1=ALU.mult)
                ins.then_inc(fin_dve, 1)
                dve.wait_ge(fin_dve, 2 * i + 2)
                dve.wait_ge(rstdy_done, i + 1)
                dve.wait_ge(h2b_done, i + 1)
                wait(dve, y_stored, 32 * i)
                for s in range(SUB):
                    ins = v.scalar_tensor_tensor(out=y_out[:, s, :], in0=acc[:, s, :], scalar=rstd_y[:, s:s + 1],
                                                 in1=h2b[:, bass.ds(i * SUB + s, 1), :].squeeze(1),
                                                 op0=ALU.mult, op1=ALU.add)
                    if s % 2 == 1:
                        ins.then_inc(y_done, 1)

            block_loop(dve, experts)

        @block.gpsimd
        def _(pool):
            g = nc.gpsimd

            for i in range(4):
                for j in range(4):
                    pool.dma_start(table[16 * j + i:16 * j + 16:4, 64:128], a["shape"]).then_inc(shape_in, 16)

            def deviation(n):
                t = slice(SUB * n, SUB * n + SUB)
                pool.wait_ge(n_mv_done, n + 1)
                g.tensor_tensor(n_var[:, t], n_mv[:, t, 1], eps.to_broadcast([TT, SUB]), ALU.add)\
                    .then_inc(n_var_done, 1)
                pool.wait_ge(n_var_done, n + 1)
                g.tensor_tensor(n_rstd[:, t], n_var[:, t], neg_half[0:TT, :].to_broadcast([TT, SUB]), ALU.pow)\
                    .then_inc(n_rstd_done, 1)

            pool.wait_ge(preset, 1)
            pool.wait_ge(early_in, 16)
            deviation(0)
            for n in range(NBLK + 1):
                if n + 1 < NBLK:
                    deviation(n + 1)
                if n >= 1:
                    u = (n - 1) % 2
                    for t in range(3):
                        pool.wait_ge(part_b, 3 * (n - 1) + t + 1)
                        g.tensor_tensor(part[u][:, 6 + t, :], rest[u][:, t, :], part[u][:, 3 + t, :],
                                        ALU.subtract).then_inc(part_c, 1)

            def split_weights(n, hi, lo, raw, hi_lo, raw_1):
                ones = one[:].to_broadcast([128, raw.shape[-1]])
                g.tensor_tensor(hi, raw, ones, ALU.mult).then_inc(w_hi_done, 1)
                g.tensor_tensor(hi_lo, raw_1, ones, ALU.mult).then_inc(w_hi_done, 1)
                pool.wait_ge(w_hi_done, 2 * n + 1)
                g.tensor_tensor(lo, raw, hi.bitcast(F32), ALU.subtract).then_inc(w_lo_done, 1)
                pool.wait_ge(w_lo_done, 2 * n + 1)
                g.tensor_tensor(hi_lo[F1:], raw_1[F1:], hi_lo[F1:].bitcast(F32), ALU.subtract).then_inc(w_lo_done, 1)
                pool.wait_ge(w_lo_done, 2 * n + 2)

            def split_chunk(n):
                if not isinstance(n, int) or n < NWCHUNK:
                    c = bass.ds(n * WCHUNK, WCHUNK)
                    split_weights(n, wd_hi[:, c], wd_lo[:, c], wd_raw[:, c], wd_1[:, c], wd_1_raw[:, c])
                elif n == NWCHUNK:
                    split_weights(n, w1_hi[:], w1_lo[:], w1_raw, w1_1[:], w1_1_raw)

            def second_deviation(n):
                pool.wait_ge(n_mv_done, NBLK + n + 1)
                g.tensor_tensor(n2_var[:], n2_mv[:, :, 1], eps.to_broadcast([TT, SUB]), ALU.add)\
                    .then_inc(n_var_done, 1)
                pool.wait_ge(n_var_done, NBLK + n + 1)
                g.tensor_tensor(n2_rstd[:], n2_var[:], neg_half[0:TT, :].to_broadcast([TT, SUB]), ALU.pow)\
                    .then_inc(n_rstd_done, 1)

            def attention(it, first, last_it):
                for j in range(PER // 2):
                    if last_it and j == PER // 2 - 1:
                        second_deviation(0)
                    pool.wait_ge(rsum2_done, PER // 2 * it + j + 1)
                    wait(pool, rsum2_tp, PER // 2 * it + j)
                    g.tensor_tensor(rsum2_rep[:].rearrange("p c j d -> p (c j) d"),
                                    rsum2[:].rearrange("p c j -> p (c j)").unsqueeze(2).to_broadcast([128, 8, 2 * D]),
                                    one[:].unsqueeze(2).to_broadcast([128, 8, 2 * D]), ALU.mult)\
                        .then_inc(rep_done, 1)
                    if not first and not last_it and j == 3:
                        pool.wait_ge(expert_w_in, 48 * it)
                        split_chunk(it - 1)
                    if last_it and 1 <= j <= 3:
                        if j == 1:
                            pool.wait_ge(expert_w_in, 48 * (NWCHUNK + 1))
                        split_chunk(NIT - 3 + j)

            looped(pool, attention)

            def add_beta(n):
                h = h2b[:, bass.ds(n * SUB, SUB), :]
                pool.wait_ge(h2_out, n + 1)
                g.tensor_tensor(h, h, beta[:].unsqueeze(1).to_broadcast([TT, SUB, C]), ALU.add).then_inc(h2b_done, 1)

            def ahead(n):
                pool.wait_ge(compared, n + 1)
                ge = cmp_ge[:].rearrange("p t e j -> p t (e j)")
                tri = earlier.rearrange("p e j -> p (e j)").unsqueeze(1).to_broadcast([TT, SUB, E * E])
                g.tensor_tensor(ge, ge, tri, ALU.mult).then_inc(ahead_done, 1)

            def exponentials(n):
                pool.wait_ge(route_dve, n + 1)
                wait(pool, gate_done, n)
                g.tensor_tensor(expl[:].rearrange("p t e -> p (t e)"), euler.to_broadcast([TT, SUB * E]),
                                shifted[:].rearrange("p t e -> p (t e)"), ALU.pow).then_inc(route_exp, 1)

            pool.wait_ge(late_in, 16 * LATE_DMAS)
            for step in (add_beta, ahead, exponentials):
                step(0)

            def experts(i, first, last_block):
                if not last_block:
                    for step in (second_deviation, add_beta, ahead, exponentials):
                        step(i + 1)
                pool.wait_ge(mv_done, i + 1)
                g.tensor_tensor(vy[:], mv[:, :, 1], eps[:].to_broadcast([TT, SUB]), ALU.add).then_inc(vy_done, 1)
                pool.wait_ge(vy_done, i + 1)
                g.tensor_tensor(rstd_y[:], vy[:], neg_half[0:TT, :].to_broadcast([TT, SUB]), ALU.pow)\
                    .then_inc(rstdy_done, 1)

            block_loop(pool, experts)


def constants():
    f = np.float32
    q = np.arange(128)
    k = np.arange(N)
    def mask(rows):
        return np.where((rows % NUM)[:, None] == (k % NUM)[None, :], f(0.5), f(1.0)).astype(f)
    pos = np.arange(NT, dtype=f)[:, None]
    inv = np.exp(-(np.arange(0, C, 2, dtype=f) / f(C)) * f(np.log(10000.0))).astype(f)
    ang = (pos * inv).astype(f)
    pe = np.stack([np.sin(ang), np.cos(ang)], axis=-1).reshape(NT, C).astype(f)
    scale = np.where(np.arange(2 * C) < C, f(D) ** f(-0.5), f(1.0)).astype(f)
    e = np.arange(E)
    return {
        "iota": np.arange(VOC, dtype=f)[:, None],
        "pe": pe.T.reshape(2, CP, NT).transpose(1, 0, 2),
        "eps": np.full((TT, 1), LN_EPS, f),
        "neg_half": np.full((128, 1), -0.5, f),
        "qk_scale": scale.reshape(3, 128).T,
        "ident": np.eye(128, dtype=f),
        "mask_a": mask(q),
        "mask_b": mask(128 + q % 64),
        "mask_r": np.roll(mask(q), REST, axis=1),
        "earlier": np.broadcast_to((e[None, :] < e[:, None]).astype(f), (TT, E, E)),
        "euler": np.full((TT, 1), np.e, f),
        "later": np.broadcast_to((E - 1 - e).astype(f), (TT, E)),
    }


def kernel(**inputs):
    import concourse.bacc as bacc
    from concourse.bass_utils import run_bass_kernel_spmd

    i = {k: np.asarray(v) for k, v in inputs.items()}

    def chunks(w):
        return w.reshape(2, CP, -1).transpose(1, 0, 2)

    w_o = np.zeros((4, 32, GROUPS, C), np.float32)
    w_o[:, :D] = i["L0_attn_w_out"].T.reshape(GROUPS, 4, D, C).transpose(1, 2, 0, 3)
    w_down = i["L0_ffn_down_w"].transpose(1, 0, 2).reshape(C, E * ED)
    fields = {
        "w_qk": chunks(i["L0_attn_w_qkv"][:2 * C].T), "w_v": chunks(i["L0_attn_w_qkv"][2 * C:].T),
        "w_o": w_o, "b_o": i["L0_attn_b_out"].reshape(2, CP).T, "b1": i["L0_ffn_b1"].reshape(CP, 1),
        "w2": i["L0_ffn_w2"], "down_b": i["L0_ffn_down_b"].reshape(2 * E, 128).T,
        **constants(),
    }

    def packed(names):
        out = np.zeros((128, sum(words(s) for _, s in names)), np.float32)
        at = 0
        for name, shape in names:
            out[:shape[0], at:at + words(shape)] = fields[name].reshape(shape[0], -1)
            at += words(shape)
        return out

    arrays = {
        "x_patch": i["x"].reshape(B, 3, 7, 2, 8, 7, 16).transpose(4, 6, 1, 3, 0, 2, 5).reshape(128, KP, NPATCH),
        "w_tok": i["L0_tok_W"].reshape(C, 2, 8, 16, 3).transpose(2, 3, 4, 1, 0).reshape(128, KP, C),
        "b_tok": i["L0_tok_b"].reshape(2, CP).T,
        "tokens": i["x_txt"].reshape(B * NT),
        "color": i["L0_txt_color_W"], "shape": i["L0_txt_shape_W"],
        "quantity": i["L0_txt_quantity_W"], "special": i["L0_txt_special_W"],
        "w1_0": i["L0_ffn_w1"][:F0], "w1_1": i["L0_ffn_w1"][F0:], "b2": i["L0_ffn_b2"],
        "wd_0": w_down[:F0], "wd_1": w_down[F0:],
        "w_up": i["L0_ffn_up_w"].reshape(2 * E, 128, C).transpose(1, 0, 2),
        "gamma": i["L0_ffn_gamma"], "beta": i["L0_ffn_beta"],
        "iota": fields["iota"], "pe": fields["pe"],
        "early": packed(EARLY), "late": packed(LATE),
    }
    arrays = {k: np.ascontiguousarray(v) for k, v in arrays.items()}
    nc = bacc.Bacc("TRN2", target_bir_lowering=False, num_devices=1)
    aps = {k: nc.dram_tensor(f"in_{k}", v.shape, mybir.dt.from_np(v.dtype), kind="ExternalInput").ap()
           for k, v in arrays.items()}
    out = nc.dram_tensor("out", (T, C), F32, kind="ExternalOutput").ap()
    build(nc, aps, out)
    r = run_bass_kernel_spmd(nc, [{f"in_{k}": v for k, v in arrays.items()}], core_ids=[0])
    return r.results[0]["out"].reshape(B, N, C)
```
